# Optimizing a Trainium2 kernel written in Bass

```python
import numpy as np
import jax
import jax.numpy as jnp

def _softmax(x, axis=-1):
    return jax.nn.softmax(x, axis=axis)

def _gelu(x):
    return jax.nn.gelu(x, approximate=True)

def _silu(x):
    return jax.nn.silu(x)

def _sigmoid(x):
    return jax.nn.sigmoid(x)

def _layernorm(x, axis=-1, eps=1e-05):
    m = jnp.mean(x, axis=axis, keepdims=True)
    v = jnp.var(x, axis=axis, keepdims=True)
    return (x - m) / jnp.sqrt(v + eps)

def _scatter_add(tgt, idx, src, axis=0):
    return tgt.at[idx].add(src)

def _segment_sum(src, seg, n):
    return jax.ops.segment_sum(src, seg, n)
kernel_name = 'mk_early_fusion_d1_tok_img256_r4_bab89b'

def setup_inputs(seed: int=0):
    np.random.seed(seed)
    _w = jnp.asarray

    def _rec_inputs():
        import jax
        import jax.numpy as jnp
        _rk = jax.random.key(seed)
        x = 7.57192e-06 + 1.00007 * jax.random.normal(jax.random.fold_in(_rk, 1), (16, 3, 224, 224), jnp.float32)
        txt = 0.00191194 + 0.0219993 * jax.random.normal(jax.random.fold_in(_rk, 2), (16, 512, 64), jnp.float32)
        return (x, txt)
    x, txt = _rec_inputs()

    def _L0_tok_setup():
        import jax, jax.numpy as jnp
        import numpy as np
        import math
        GRID = 28
        NUM_PATCHES = GRID * GRID
        PATCH = 8
        IN_CH = 3
        HIDDEN = 64
        BATCH = 64

        def build_grid_edges():
            edges = []
            for i in range(GRID):
                for j in range(GRID):
                    cur = i * GRID + j
                    if j < GRID - 1:
                        edges.append([cur, cur + 1])
                    if i < GRID - 1:
                        edges.append([cur, cur + GRID])
            e = np.asarray(edges, dtype=np.int32).T
            e = np.concatenate([e, e[::-1]], axis=1)
            return jnp.asarray(e)

        def sin_positional_encoding(n, d):
            pos = jnp.arange(n, dtype=jnp.float32)[:, None]
            div = jnp.exp(jnp.arange(0, d, 2, dtype=jnp.float32) * (-math.log(10000.0) / d))
            pe = jnp.zeros((n, d), dtype=jnp.float32)
            pe = pe.at[:, 0::2].set(jnp.sin(pos * div))
            pe = pe.at[:, 1::2].set(jnp.cos(pos * div))
            return pe
        key = jax.random.key(seed)
        ks = jax.random.split(key, 8)
        s = 0.02
        return {'x': jax.random.normal(ks[0], (BATCH, IN_CH, 224, 224), dtype=jnp.float32), 'W_embed': jax.random.normal(ks[1], (IN_CH * PATCH * PATCH, HIDDEN), dtype=jnp.float32) * s, 'b_embed': jax.random.normal(ks[2], (HIDDEN,), dtype=jnp.float32) * s, 'W_gcn': jax.random.normal(ks[3], (3, HIDDEN, HIDDEN), dtype=jnp.float32) * s, 'b_gcn': jax.random.normal(ks[4], (3, HIDDEN), dtype=jnp.float32) * s, 'W_out': jax.random.normal(ks[5], (HIDDEN, 64), dtype=jnp.float32) * s, 'b_out': jax.random.normal(ks[6], (64,), dtype=jnp.float32) * s, 'edge_index': build_grid_edges()}
    _L0_tok_all = _L0_tok_setup()
    _L0_tok_in = {k: v for k, v in _L0_tok_all.items() if k in ('W_embed', 'b_embed', 'W_gcn', 'b_gcn', 'W_out', 'b_out', 'edge_index')}
    del _L0_tok_all

    def _L0_attn_setup():
        import jax, jax.numpy as jnp
        import numpy as np
        import math
        PI = math.pi

        def _encode_phase(x, w1, b1, w2, b2):
            h = jnp.tanh(jnp.einsum('bld,ed->ble', x, w1) + b1)
            return jnp.tanh(jnp.einsum('bld,kd->blk', h, w2) + b2) * PI
        key = jax.random.key(seed)
        ks = jax.random.split(key, 12)
        B, L, D, K = (2, 512, 64, 32)
        s = 0.02
        return {'x': jax.random.normal(ks[0], (B, L, D), dtype=jnp.float32), 'kw1': jax.random.normal(ks[1], (D, D), dtype=jnp.float32) * s, 'kb1': jnp.zeros((D,), dtype=jnp.float32), 'kw2': jax.random.normal(ks[2], (K, D), dtype=jnp.float32) * s, 'kb2': jnp.zeros((K,), dtype=jnp.float32), 'qw1': jax.random.normal(ks[3], (D, D), dtype=jnp.float32) * s, 'qb1': jnp.zeros((D,), dtype=jnp.float32), 'qw2': jax.random.normal(ks[4], (K, D), dtype=jnp.float32) * s, 'qb2': jnp.zeros((K,), dtype=jnp.float32), 'vw': jax.random.normal(ks[5], (D, D), dtype=jnp.float32) * s, 'vb': jnp.zeros((D,), dtype=jnp.float32)}
    _L0_attn_all = _L0_attn_setup()
    _L0_attn_in = {k: v for k, v in _L0_attn_all.items() if k in ('kw1', 'kb1', 'kw2', 'kb2', 'qw1', 'qb1', 'qw2', 'qb2', 'vw', 'vb')}
    del _L0_attn_all

    def _L0_ffn_setup():
        import math
        import jax, jax.numpy as jnp
        import numpy as np
        CAPACITY_FACTOR = 1.25
        key = jax.random.key(seed)
        ks = jax.random.split(key, 5)
        B, L, D, F, E = (8, 2048, 64, 256, 8)
        h = jax.random.normal(ks[0], (B, L, D), dtype=jnp.float32)
        gate_w = jax.random.normal(ks[1], (D, E), dtype=jnp.float32) * 0.02
        gate_b = jnp.zeros((E,), dtype=jnp.float32)
        w1 = jax.random.normal(ks[2], (E, D, F), dtype=jnp.float32) * (1.0 / math.sqrt(D))
        b1 = jnp.zeros((E, F), dtype=jnp.float32)
        w2 = jax.random.normal(ks[3], (E, F, D), dtype=jnp.float32) * (1.0 / math.sqrt(F))
        b2 = jnp.zeros((E, D), dtype=jnp.float32)
        return {'h': h, 'gate_w': gate_w, 'gate_b': gate_b, 'w1': w1, 'b1': b1, 'w2': w2, 'b2': b2}
    _L0_ffn_all = _L0_ffn_setup()
    _L0_ffn_in = {k: v for k, v in _L0_ffn_all.items() if k in ('gate_w', 'gate_b', 'w1', 'b1', 'w2', 'b2')}
    del _L0_ffn_all
    return {'x': x, 'txt': txt, 'L0_tok_W_embed': _L0_tok_in['W_embed'], 'L0_tok_b_embed': _L0_tok_in['b_embed'], 'L0_tok_W_gcn': _L0_tok_in['W_gcn'], 'L0_tok_b_gcn': _L0_tok_in['b_gcn'], 'L0_tok_W_out': _L0_tok_in['W_out'], 'L0_tok_b_out': _L0_tok_in['b_out'], 'L0_tok_edge_index': _L0_tok_in['edge_index'], 'L0_attn_kw1': _L0_attn_in['kw1'], 'L0_attn_kb1': _L0_attn_in['kb1'], 'L0_attn_kw2': _L0_attn_in['kw2'], 'L0_attn_kb2': _L0_attn_in['kb2'], 'L0_attn_qw1': _L0_attn_in['qw1'], 'L0_attn_qb1': _L0_attn_in['qb1'], 'L0_attn_qw2': _L0_attn_in['qw2'], 'L0_attn_qb2': _L0_attn_in['qb2'], 'L0_attn_vw': _L0_attn_in['vw'], 'L0_attn_vb': _L0_attn_in['vb'], 'L0_ffn_gate_w': _L0_ffn_in['gate_w'], 'L0_ffn_gate_b': _L0_ffn_in['gate_b'], 'L0_ffn_w1': _L0_ffn_in['w1'], 'L0_ffn_b1': _L0_ffn_in['b1'], 'L0_ffn_w2': _L0_ffn_in['w2'], 'L0_ffn_b2': _L0_ffn_in['b2']}

def reference(x, txt, L0_tok_W_embed, L0_tok_b_embed, L0_tok_W_gcn, L0_tok_b_gcn, L0_tok_W_out, L0_tok_b_out, L0_tok_edge_index, L0_attn_kw1, L0_attn_kb1, L0_attn_kw2, L0_attn_kb2, L0_attn_qw1, L0_attn_qb1, L0_attn_qw2, L0_attn_qb2, L0_attn_vw, L0_attn_vb, L0_ffn_gate_w, L0_ffn_gate_b, L0_ffn_w1, L0_ffn_b1, L0_ffn_w2, L0_ffn_b2):
    import jax
    import jax.numpy as jnp

    def _L0_tok_ref(x, W_embed, b_embed, W_gcn, b_gcn, W_out, b_out, edge_index):
        import jax, jax.numpy as jnp
        import numpy as np
        import math
        GRID = 28
        NUM_PATCHES = GRID * GRID
        PATCH = 8
        IN_CH = 3
        HIDDEN = 64
        BATCH = 64

        def build_grid_edges():
            edges = []
            for i in range(GRID):
                for j in range(GRID):
                    cur = i * GRID + j
                    if j < GRID - 1:
                        edges.append([cur, cur + 1])
                    if i < GRID - 1:
                        edges.append([cur, cur + GRID])
            e = np.asarray(edges, dtype=np.int32).T
            e = np.concatenate([e, e[::-1]], axis=1)
            return jnp.asarray(e)

        def sin_positional_encoding(n, d):
            pos = jnp.arange(n, dtype=jnp.float32)[:, None]
            div = jnp.exp(jnp.arange(0, d, 2, dtype=jnp.float32) * (-math.log(10000.0) / d))
            pe = jnp.zeros((n, d), dtype=jnp.float32)
            pe = pe.at[:, 0::2].set(jnp.sin(pos * div))
            pe = pe.at[:, 1::2].set(jnp.cos(pos * div))
            return pe
        B = x.shape[0]
        N = NUM_PATCHES
        p = x.reshape(B, IN_CH, GRID, PATCH, GRID, PATCH)
        p = p.transpose(0, 2, 4, 1, 3, 5).reshape(B, N, IN_CH * PATCH * PATCH)
        h = p @ W_embed + b_embed + sin_positional_encoding(N, HIDDEN)[None]
        src, dst = (edge_index[0], edge_index[1])
        deg = jnp.zeros((N,), dtype=h.dtype).at[dst].add(1.0) + 1.0
        dinv = deg ** (-0.5)
        enorm = (dinv[src] * dinv[dst])[None, :, None]
        snorm = (1.0 / deg)[None, :, None]
        for i in range(3):
            hw = h @ W_gcn[i]
            agg = hw * snorm
            agg = agg.at[:, dst].add(hw[:, src] * enorm)
            h = jax.nn.relu(agg + b_gcn[i])
        return h @ W_out + b_out

    def _L0_attn_ref(x, kw1, kb1, kw2, kb2, qw1, qb1, qw2, qb2, vw, vb):
        import jax, jax.numpy as jnp
        import numpy as np
        import math
        PI = math.pi

        def _encode_phase(x, w1, b1, w2, b2):
            h = jnp.tanh(jnp.einsum('bld,ed->ble', x, w1) + b1)
            return jnp.tanh(jnp.einsum('bld,kd->blk', h, w2) + b2) * PI
        B, L, D = x.shape
        key_phase = _encode_phase(x, kw1, kb1, kw2, kb2)
        query_phase = _encode_phase(x, qw1, qb1, qw2, qb2)
        K = key_phase.shape[-1]
        value = jnp.einsum('bld,ed->ble', x, vw) + vb
        cos_k = jnp.cos(key_phase)[..., None]
        sin_k = jnp.sin(key_phase)[..., None]
        v_exp = value[:, :, None, :]
        mem_real = jnp.cumsum(cos_k * v_exp, axis=1)
        mem_imag = jnp.cumsum(sin_k * v_exp, axis=1)
        cos_q = jnp.cos(query_phase)[..., None]
        sin_q = jnp.sin(query_phase)[..., None]
        retrieved = jnp.sum(mem_real * cos_q + mem_imag * sin_q, axis=2)
        positions = jnp.arange(1, L + 1, dtype=x.dtype)
        norm = jnp.sqrt(positions * K)[None, :, None]
        return retrieved / norm

    def _L0_ffn_ref(h, gate_w, gate_b, w1, b1, w2, b2):
        import math
        import jax, jax.numpy as jnp
        import numpy as np
        CAPACITY_FACTOR = 1.25
        B, L, D = h.shape
        E = gate_w.shape[1]
        T = B * L
        C = max(1, math.ceil(CAPACITY_FACTOR * T / E))
        x = h.reshape(T, D)
        logits = x @ gate_w + gate_b
        probs = jax.nn.softmax(logits, axis=-1)
        idx = jnp.argmax(probs, axis=-1)
        prb = jnp.take_along_axis(probs, idx[:, None], axis=1)[:, 0]
        one_hot = jax.nn.one_hot(idx, E, dtype=jnp.float32)
        pos = (jnp.cumsum(one_hot, axis=0) * one_hot).sum(-1).astype(jnp.int32) - 1
        kept = pos < C
        pos_safe = jnp.where(kept, pos, C)
        buf = jnp.zeros((E, C, D), dtype=h.dtype).at[idx, pos_safe].set(x, mode='drop')
        hmid = jax.nn.relu(jnp.einsum('ecd,edf->ecf', buf, w1) + b1[:, None, :])
        ybuf = jnp.einsum('ecf,efd->ecd', hmid, w2) + b2[:, None, :]
        pos_g = jnp.minimum(pos, C - 1)
        y_tok = ybuf[idx, pos_g] * (prb * kept)[:, None]
        y = y_tok.reshape(B, L, D)
        y = jnp.nan_to_num(y, nan=0.0, posinf=10000.0, neginf=-10000.0)
        return y
    h = _L0_tok_ref(x, L0_tok_W_embed, L0_tok_b_embed, L0_tok_W_gcn, L0_tok_b_gcn, L0_tok_W_out, L0_tok_b_out, L0_tok_edge_index)
    h = jnp.concatenate([h, txt], axis=1)
    h = h + _L0_attn_ref(_layernorm(h, axis=-1), L0_attn_kw1, L0_attn_kb1, L0_attn_kw2, L0_attn_kb2, L0_attn_qw1, L0_attn_qb1, L0_attn_qw2, L0_attn_qb2, L0_attn_vw, L0_attn_vb)
    h = h + _L0_ffn_ref(_layernorm(h, axis=-1), L0_ffn_gate_w, L0_ffn_gate_b, L0_ffn_w1, L0_ffn_b1, L0_ffn_w2, L0_ffn_b2)
    return h

_drawn_inputs = setup_inputs


def setup_inputs(seed=0):
    import zlib

    import numpy as np

    out = dict(_drawn_inputs(seed))
    spreads = {'L0_attn_kb1': (0.0, 0.8),
     'L0_attn_kb2': (0.0, 0.1),
     'L0_attn_qb1': (0.0, 0.8),
     'L0_attn_qb2': (0.0, 0.1),
     'L0_attn_vb': (0.0, 0.1),
     'L0_ffn_gate_b': (0.0, 0.8),
     'L0_ffn_b1': (0.0, 0.8),
     'L0_ffn_b2': (0.0, 2.0)}
    factors = {'x': 8.0,
     'txt': 5.263,
     'L0_tok_W_embed': 8.0,
     'L0_tok_b_embed': 8.0,
     'L0_tok_W_gcn': 4.24,
     'L0_attn_kw1': 8.0,
     'L0_attn_kw2': 8.0,
     'L0_attn_qw1': 8.0,
     'L0_attn_qw2': 8.0,
     'L0_ffn_gate_w': 8.0,
     'L0_ffn_w1': 8.0,
     'L0_ffn_w2': 8.0}
    for name, (base, spread) in spreads.items():
        noise = np.random.default_rng([zlib.crc32(name.encode()), seed]).standard_normal(out[name].shape)
        drawn = base * np.exp(spread * noise) if base else spread * noise
        out[name] = jnp.asarray(drawn.astype(out[name].dtype))
    for name, factor in factors.items():
        out[name] = (out[name] * factor).astype(out[name].dtype)
    return out
```

```python
import concourse.bass as bass
from concourse import mybir
from contextlib import ExitStack

F32 = mybir.dt.float32
F16 = mybir.dt.float16
I32 = mybir.dt.int32
ALU = mybir.AluOpType
ACT = mybir.ActivationFunctionType
AX = mybir.AxisListType

P = 128
BATCH = 16
PAIRS = BATCH // 2
D = 64
GRID = 28
PATCH = 8
CHANNELS = 3
SIDE = GRID * PATCH
NODES = GRID * GRID
TEXT = 512
L = NODES + TEXT
EDGES = 2 * 2 * GRID * (GRID - 1)
LAYERS = 3
PHASES = 32
EXPERTS = 8
HIDDEN = 256
TOKENS = BATCH * L
CAPACITY = -(-5 * TOKENS // (4 * EXPERTS))
LN_EPS = 1e-5
RSQRT_SEED = float(0x5F3759DF)
PI = 3.141592653589793

NODE_CHUNK, NODE_CHUNKS = 112, NODES // 112
TEXT_CHUNK, TEXT_CHUNKS = 128, TEXT // 128
CHUNKS = NODE_CHUNKS + TEXT_CHUNKS
ROWS = 2 * CHUNKS
GROUPS = [(0, 4, 112, 0), (4, 7, 112, 448), (7, 11, 128, 784)]
SCORE_FILLS = [(0, 1), (2, 3), (4, 5), (6,), (7, 8), (9, 10)]
EDGE_P = 126
EDGE_CHUNKS = EDGES // EDGE_P
EDGE_UNROLL = 4

ROW = 132
ROW_H, ROW_PRB, ROW_TOK = D, 2 * D, 2 * D + 1
NOWHERE = 1 << 20

TILE = 120
TILES = CAPACITY // TILE
STEP_TILES = 3
STEPS = TILES // STEP_TILES
STEP_COLS = STEP_TILES * TILE
EXPERT_PAIRS = EXPERTS // 2
SLOTS = 3
TURNS = STEPS // SLOTS

TOK_USES = ["embed", "hw0", "agg0", "hw1", "agg1", "hw2", "agg2", "out"]
ATT_USES = ["xnT", "q1", "k1", "v", "q2", "k2", "kT", "kv", "out", "xn2T"]

WEIGHT_LOADS = 12 + 2 * (LAYERS + 4 + 4 + 1 + 6 + 4 + 3)
ZEROED = 6
BASE = {0: 8 * PAIRS, 1: 8 * PAIRS, 2: 10 * PAIRS, 3: 10 * PAIRS, 4: 10 * PAIRS, 5: 4 * PAIRS}
LOOP_STEPS = 134
FFN_LOOP_STEPS = 21

_widths = [("ident", P), ("causal", P), ("position", NODES), ("nodes", NODES), ("rnorm", CHUNKS),
           ("expert_less_8", EXPERTS), ("slot_base", EXPERTS), ("carry", EXPERTS * ROWS), ("token", ROWS),
           ("fold", 1), ("sin_scale", 1), ("sin_bias", 1), ("block_start", NODE_CHUNKS)]
CONST = {}
_at = 0
for _n, _w in _widths:
    CONST[_n] = (_at, _at + _w)
    _at += _w
CONST_COLS = _at


def first_token(chunk):
    return chunk * NODE_CHUNK if chunk < NODE_CHUNKS else NODES + (chunk - NODE_CHUNKS) * TEXT_CHUNK


def tokens_in(chunk):
    return NODE_CHUNK if chunk < NODE_CHUNKS else TEXT_CHUNK


def later(step, k):
    ep, i, u = step
    i, u = i + (u + k) // SLOTS, (u + k) % SLOTS
    if isinstance(i, int) and i >= TURNS:
        ep, i = ep + 1, i - TURNS
    return (ep, i, u) if ep < EXPERT_PAIRS else None


def number(step):
    ep, i, u = step
    return (i + ep * TURNS) * SLOTS + u


def wait_apart(eng, sem, value, waits):
    eng.wait_ge(sem, value)
    eng.sem_inc(waits, 1)


class Steps:

    def __init__(self, eng, sem):
        self.eng, self.sem, self.base, self.n = eng, sem, 0, 0

    def done(self, ins):
        self.n += 1
        ins.then_inc(self.sem, 1)

    def settle(self):
        self.eng.wait_ge(self.sem, self.base + self.n)

    def begin(self, base):
        self.base, self.n = base, 0


def build(nc, d):
    ctx = ExitStack()
    with ctx:
        def sb(name, shape, dt=F32):
            return ctx.enter_context(nc.sbuf_tensor("sb_" + name, shape, dt))

        def sem(name):
            return ctx.enter_context(nc.semaphore(name))

        slots = nc.dram_tensor("expert_slots", [EXPERTS * CAPACITY, ROW], F32, kind="Internal").ap()
        out = d["out"].rearrange("b l d -> (b l) d")

        const = sb("const", [P, CONST_COLS])

        def cst(name, p=P):
            return const[0:p, CONST[name][0]:CONST[name][1]]

        causal16 = sb("causal16", [P, P], F16)
        ones16 = sb("ones16", [P, P], F16)
        ones = sb("ones", [P, P])
        embed_w = sb("embed_w", [96, 4, P])
        gcn_w = sb("gcn_w", [P, LAYERS, P])
        out_w = sb("out_w", [P, P])
        q1_w, k1_w, v_w = sb("q1_w", [P, P]), sb("k1_w", [P, P]), sb("v_w", [P, P])
        q2_w, k2_w = sb("q2_w", [P, P]), sb("k2_w", [P, P])
        gate_w = sb("gate_w", [P, 2 * EXPERTS])
        bias = sb("bias", [P, 8])
        b1_col = sb("b1_col", [P, EXPERTS, 2])
        out_b, v_b = sb("out_b", [P, 2, D]), sb("v_b", [P, 2, D])
        gate_b = sb("gate_b", [P, 2, EXPERTS])
        b2_row = sb("b2_row", [P, EXPERTS, D])
        w1 = sb("w1", [P, EXPERT_PAIRS, 2, HIDDEN])
        w2 = sb("w2", [P, EXPERTS, 2, P])
        adj = sb("adj", [NODE_CHUNK, NODE_CHUNKS, NODES])
        pos_b = sb("pos_b", [P, NODES])

        image = sb("image", [96, GRID, SIDE])
        hT = sb("hT", [P, NODES])
        hw = sb("hw", [NODE_CHUNK, NODE_CHUNKS, P])
        h0 = sb("h0", [P, CHUNKS, 2, D])
        xn = sb("xn", [P, CHUNKS, 2, D])
        xnT = sb("xnT", [P, L])
        h1q, h1k = sb("h1q", [P, L]), sb("h1k", [P, L])
        tq, tk = sb("tq", [P, L]), sb("tk", [P, L])
        phq, phk = sb("phq", [P, L]), sb("phk", [P, L])
        phq_pad = sb("phq_pad", [P, 2, L])
        phk_tok = sb("phk_tok", [P, CHUNKS, P])
        xn2 = phk_tok
        v_pad = sb("v_pad", [P, CHUNKS, 4, D])
        state = sb("state", [P, CHUNKS, P])
        masked = sb("masked", [P, 3, 4, P])
        rows = sb("rows", [P, ROWS, ROW])
        small = sb("small", [P, 24, ROWS])
        stats = sb("stats", [P, ROWS, 6])
        route = sb("route", [P, 8, ROWS * EXPERTS])
        onehot16 = sb("onehot16", [P, ROWS * EXPERTS], F16)
        base = sb("base", [P, EXPERTS])
        slot_idx = sb("slot_idx", [P, ROWS], I32)
        far_edges = sb("far_edges", [1, 1], I32)
        near_sum = sb("near_sum", [NODE_CHUNK, NODE_CHUNKS])
        far_sum = sb("far_sum", [NODE_CHUNK, NODE_CHUNKS + 1])
        junk, junk2 = sb("junk", [P, 1]), sb("junk2", [P, 1])

        nodes16 = hT[:, 0:NODES // 2].bitcast(F16)
        ident16 = sb("ident16", [P, P], F16)
        edges_i = sb("edges_i", [EDGE_P, 2, EDGE_CHUNKS], I32)
        edges_f = sb("edges_f", [EDGE_P, 2, EDGE_CHUNKS])
        hot_src = phq_pad[:, :, :].rearrange("p a b -> p (a b)")[:, 0:EDGE_UNROLL * NODES // 2].bitcast(F16)\
            .rearrange("p (u n) -> p u n", u=EDGE_UNROLL)
        hot_dst = v_pad[:, :, :, :].rearrange("p a b c -> p (a b c)")[:, 0:EDGE_UNROLL * NODES // 4].bitcast(F16)\
            .rearrange("p (u n) -> p u n", u=EDGE_UNROLL)
        self_loop = [rows[0:NODE_CHUNK, :, :].rearrange("p a b -> p (a b)")[:, 1372 * k:1372 * k + 1372].bitcast(F16)
                     .rearrange("p (s n) -> p s n", s=NODE_CHUNKS) for k in range(2)]
        diag = phk_tok[0:NODE_CHUNK, 0:NODE_CHUNKS, 0:NODE_CHUNK]
        blank = image[:, :, :].rearrange("p a b -> p (a b)")[0:60, 0:27 * ROW].rearrange("p (n r) -> p n r", r=ROW)

        def flat(t, p, n):
            names = "abc"[0:len(t.shape) - 1]
            v = t[:, :] if len(names) == 1 else t[tuple([slice(None)] * len(t.shape))].rearrange(
                f"p {' '.join(names)} -> p ({' '.join(names)})")
            return v[0:p, 0:n]

        expert_xn = [sb(f"expert_xn{u}", [TILE, STEP_TILES, 2, D]) for u in range(SLOTS)]
        expert_rows = [sb(f"expert_rows{u}", [TILE, 2, STEP_TILES, ROW - D]) for u in range(SLOTS)]
        xT = [t[:, 0:STEP_COLS] for t in (xnT, h1q, h1k)]
        mid = [flat(t, P, 4 * STEP_COLS).rearrange("p (v h n) -> p v h n", v=2, h=2) for t in (phq_pad, v_pad, masked)]
        y_work = [flat(t, TILE, 2 * STEP_TILES * D).rearrange("p (v n d) -> p v n d", v=2, d=D)
                  for t in (tq, tk, phq, phk)]
        y_out = [flat(h0, TILE, CHUNKS * P)[:, 384 * u:384 * u + 384].rearrange("p (v n d) -> p v n d", v=2, d=D)
                 for u in range(SLOTS)]
        y_token = [sb(f"y_token{u}", [TILE, 2 * STEP_TILES], I32) for u in range(SLOTS)]
        TB, HB, YB = 7, [0, 1, 2, 3], [4, 5]

        bank = [ctx.enter_context(nc.psum_tensor(f"bank{i}", [P, 512], F32)) for i in range(8)]
        A, X, S = [0, 1], [2, 3, 4], [5, 6]

        filled = [sem(f"filled_bank{i}") for i in range(8)]
        drained = [sem(f"drained_bank{i}") for i in range(8)]
        consts_loaded = sem("consts_loaded")
        weights_loaded = sem("weights_loaded")
        expert_w_loaded = sem("expert_w_loaded")
        edges_loaded = sem("edges_loaded")
        image_loaded = sem("image_loaded")
        text_loaded = sem("text_loaded")
        zeroed = sem("zeroed")
        blank_ready = sem("blank_ready")
        blank_written = sem("blank_written")
        dve_steps = sem("dve_steps")
        hot_ready = sem("hot_ready")
        hot_used = sem("hot_used")
        self_ready = sem("self_ready")
        counts_drained = sem("counts_drained")
        degree_filled = sem("degree_filled")
        diag_ready = sem("diag_ready")
        dinv_filled = sem("dinv_filled")
        far_ready, far_filled, far_known = sem("far_ready"), sem("far_filled"), sem("far_known")
        adj_ready = sem("adj_ready")
        xn_ready = sem("xn_ready")
        folded = sem("folded")
        phq_ready = sem("phq_ready")
        phk_ready = sem("phk_ready")
        phq_padded = sem("phq_padded")
        xn2_ready = sem("xn2_ready")
        xn2_in_rows = sem("xn2_in_rows")
        shifted_ready = sem("shifted_ready")
        exp_ready = sem("exp_ready")
        onehot_ready = sem("onehot_ready")
        slots_ready = sem("slots_ready")
        rows_scattered = sem("rows_scattered")
        h1_written = sem("h1_written")
        rows_free = sem("rows_free")
        expert_xn_loaded = [sem(f"expert_xn_loaded{u}") for u in range(SLOTS)]
        rows_loaded = [sem(f"rows_loaded{u}") for u in range(SLOTS)]
        y_ready = sem("y_ready")
        y_scattered = [sem(f"y_scattered{u}") for u in range(SLOTS)]
        pool_steps = sem("pool_steps")
        pool_waits, dve_waits = sem("pool_waits"), sem("dve_waits")

        block = ctx.enter_context(nc.Block())

        def att_filled(eng, q, use, g):
            eng.wait_ge(filled[X[g]], q * len(ATT_USES) + ATT_USES.index(use) + 1)

        def att_free(eng, q, use, g):
            eng.wait_ge(drained[X[g]], q * len(ATT_USES) + ATT_USES.index(use) + 1)

        def att_drained(eng, q, use, g):
            eng.wait_ge(drained[X[g]], q * len(ATT_USES) + ATT_USES.index(use) + 2)

        def tok_filled(eng, p, use, h):
            eng.wait_ge(filled[A[h]], p * len(TOK_USES) + TOK_USES.index(use) + 1)

        def tok_free(eng, p, use, h):
            eng.wait_ge(drained[A[h]], p * len(TOK_USES) + TOK_USES.index(use) + 1)

        def score_filled(eng, q, f):
            eng.wait_ge(filled[S[f % 2]], q * 4 + f // 2 + 1)

        def score_free(eng, q, f):
            eng.wait_ge(drained[S[f % 2]], q * 4 + f // 2 + 1)

        def score_drained(eng, q, f):
            eng.wait_ge(drained[S[f % 2]], q * 4 + f // 2 + 2)

        def score_view(f, n):
            return bank[S[f % 2]][0:n, :].rearrange("p (k n) -> p k n", n=P)[:, :, 0:n]

        HALVES = [(0, 4, 0, 448), (4, 7, 448, 336)]

        @block.sync
        def _(sp):
            sp.dma_start(const[:, :], d["constants"]).then_inc(consts_loaded, 16)
            sp.dma_start(edges_i[:, :, :], d["edge_index"].rearrange("t (p c) -> p t c", p=EDGE_P))\
                .then_inc(edges_loaded, 16)
            sp.wait_ge(zeroed, 1)
            w = d["W_embed"].rearrange("(c i m s) h -> s c i m h", c=CHANNELS, i=PATCH, s=2)
            for s in range(2):
                for b in range(2):
                    for c in range(CHANNELS):
                        row = 48 * s + 24 * b + 8 * c
                        sp.dma_start(embed_w[row:row + PATCH, :, b * D:b * D + D], w[s, c]).then_inc(weights_loaded, 16)
            for b in range(2):
                half = slice(b * D, b * D + D)
                for l in range(LAYERS):
                    sp.dma_start(gcn_w[half, l, half], d["W_gcn"][l]).then_inc(weights_loaded, 16)
                for tile, name in ((out_w, "W_out"), (q1_w, "qw1T"), (k1_w, "kw1T"), (v_w, "vwT")):
                    sp.dma_start(tile[half, half], d[name]).then_inc(weights_loaded, 16)
                for tile, name in ((q2_w, "qw2T"), (k2_w, "kw2T")):
                    for r in range(2):
                        at = b * D + r * PHASES
                        sp.dma_start(tile[half, at:at + PHASES], d[name]).then_inc(weights_loaded, 16)
                sp.dma_start(gate_w[half, b * EXPERTS:(b + 1) * EXPERTS], d["gate_w"]).then_inc(weights_loaded, 16)
                cols = [d["b_embed"]] + [d["b_gcn"][l] for l in range(LAYERS)] + [d["qb1"], d["kb1"]]
                for i, v in enumerate(cols):
                    sp.dma_start(bias[half, i:i + 1], v.unsqueeze(1)).then_inc(weights_loaded, 16)
                for i, name in ((6, "qb2"), (7, "kb2")):
                    for r in range(2):
                        at = b * D + r * PHASES
                        sp.dma_start(bias[at:at + PHASES, i:i + 1], d[name].unsqueeze(1)).then_inc(weights_loaded, 16)
                for tile, name in ((out_b, "b_out"), (v_b, "vb"), (gate_b, "gate_b")):
                    sp.dma_start(tile[:, b, :], d[name].partition_broadcast(P)).then_inc(weights_loaded, 16)

            sp.wait_ge(blank_ready, 1)
            for e in range(EXPERTS):
                for h in range(2):
                    n = CAPACITY // 2
                    part = slots[e * CAPACITY + h * n:e * CAPACITY + (h + 1) * n, :]
                    sp.dma_start(part.rearrange("(p n) r -> p n r", p=60), blank).then_inc(blank_written, 16)
            for e in range(EXPERTS):
                at = D * (e % 2)
                sp.dma_start(w1[at:at + D, e // 2, e % 2, :], d["w1"][e]).then_inc(expert_w_loaded, 16)
                sp.dma_start(w2[:, e, :, 0:D], d["w2"][e].rearrange("(h f) d -> f h d", h=2))\
                    .then_inc(expert_w_loaded, 16)
                sp.dma_start(b1_col[:, e, :], d["b1"][e].rearrange("(h f) -> f h", h=2),
                             allow_slow_non_contiguous=True).then_inc(expert_w_loaded, 16)
                sp.dma_start(b2_row[:, e, :], d["b2"][e].partition_broadcast(P)).then_inc(expert_w_loaded, 16)
            sp.wait_ge(blank_written, 2 * 16 * EXPERTS)

            def load_image(p):
                for s in range(2):
                    for b in range(2):
                        for c in range(CHANNELS):
                            row = 48 * s + 24 * b + 8 * c
                            src = d["x"][bass.ds(p * 2 + b, 1), c].rearrange("o (g i) w -> i (o g) w", i=PATCH)
                            sp.dma_start(image[row:row + PATCH, :, 0:SIDE - s], src[:, :, s:SIDE])\
                                .then_inc(image_loaded, 16)

            def load_text(p):
                for b in range(2):
                    src = d["txt"][bass.ds(p * 2 + b, 1)].rearrange("o (t p) d -> p (o t) d", p=TEXT_CHUNK)
                    sp.dma_start(h0[:, NODE_CHUNKS:, b, :], src).then_inc(text_loaded, 16)

            def store_h1(q):
                for b in range(2):
                    dst = d["out"][bass.ds(q * 2 + b, 1)]
                    src = rows[:, :, ROW_H:ROW_H + D].rearrange("p (c b) d -> p c b d", b=2)[:, :, b, :]
                    sp.dma_start(dst[:, 0:NODES].rearrange("o (c p) d -> p (o c) d", p=NODE_CHUNK),
                                 src[0:NODE_CHUNK, 0:NODE_CHUNKS]).then_inc(h1_written, 16)
                    sp.dma_start(dst[:, NODES:L].rearrange("o (c p) d -> p (o c) d", p=TEXT_CHUNK),
                                 src[:, NODE_CHUNKS:]).then_inc(h1_written, 16)

            load_image(0)
            sp.wait_ge(zeroed, 2)
            load_text(0)
            sp.wait_ge(filled[A[1]], 1)
            load_image(1)

            def around_pair(p, last_image):
                if not last_image:
                    sp.wait_ge(filled[A[1]], (p + 1) * len(TOK_USES) + 1)
                    load_image(p + 2)
                att_drained(sp, p, "out", 2)
                load_text(p + 1)
                sp.wait_ge(slots_ready, p + 1)
                store_h1(p)

            with sp.Fori(0, PAIRS - 2) as p:
                around_pair(p, False)
            around_pair(PAIRS - 2, True)
            sp.wait_ge(slots_ready, PAIRS)
            store_h1(PAIRS - 1)

            sp.wait_ge(rows_scattered, PAIRS * ROWS * 16)

            def expert_tiles(step, v):
                ep, i, u = step
                e = 2 * ep + v
                src = slots[e * CAPACITY:(e + 1) * CAPACITY, :].rearrange("(p n) r -> p n r", p=TILE)
                return src[:, bass.ds((i * SLOTS + u) * STEP_TILES, STEP_TILES), :]

            def load_xn(step):
                for v in range(2):
                    sp.dma_start(expert_xn[step[2]][:, :, v, :], expert_tiles(step, v)[:, :, 0:D])\
                        .then_inc(expert_xn_loaded[step[2]], 16)

            def load_rows(step):
                for v in range(2):
                    sp.dma_start(expert_rows[step[2]][:, v, :, :], expert_tiles(step, v)[:, :, D:ROW])\
                        .then_inc(rows_loaded[step[2]], 16)

            def load_ahead(step):
                if later(step, SLOTS):
                    sp.wait_ge(filled[TB], number(step) + 1)
                    load_xn(later(step, SLOTS))
                if later(step, 1):
                    sp.wait_ge(y_ready, number(step) - 1)
                    load_rows(later(step, 1))

            for u in range(SLOTS):
                load_xn((0, 0, u))
                load_rows((0, 0, u))
            for u in range(2):
                sp.wait_ge(filled[TB], u + 1)
                load_xn((0, 1, u))
            load_ahead((0, 0, 2))
            for ep in range(EXPERT_PAIRS):
                first = 1 if ep == 0 else 0
                with sp.Fori(first, TURNS - 1) as i:
                    for u in range(SLOTS):
                        load_ahead((ep, i, u))
                for u in range(SLOTS):
                    load_ahead((ep, TURNS - 1, u))

        @block.gpsimd
        def _(pool):
            for t in (embed_w, gcn_w, out_w, q1_w, k1_w, v_w, q2_w, k2_w):
                pool.memset(flat(t, t.shape[0], t.shape[1] * (t.shape[2] if len(t.shape) > 2 else 1)), 0.0)
            pool.memset(w1[:, :, :, :].rearrange("p a b c -> p (a b c)"), 0.0)
            pool.memset(w2[:, :, :, :].rearrange("p a b c -> p (a b c)"), 0.0)
            pool.memset(gate_w[:, :], 0.0).then_inc(zeroed, 1)
            pool.memset(h0[:, :, :, :].rearrange("p a b c -> p (a b c)"), 0.0).then_inc(zeroed, 1)
            pool.memset(blank, 0.0).then_inc(pool_steps, 1)
            pool.wait_ge(pool_steps, 1)
            pool.memset(blank[:, :, ROW_TOK:ROW_TOK + 1].bitcast(I32), NOWHERE).then_inc(blank_ready, 1)
            pool.memset(state[:, :, :].rearrange("p a b -> p (a b)"), 0.0).then_inc(zeroed, 1)
            pool.wait_ge(hot_used, 2 * EDGE_CHUNKS)
            pool.memset(phq_pad[:, :, :].rearrange("p a b -> p (a b)"), 0.0).then_inc(zeroed, 1)
            pool.memset(v_pad[:, :, :, :].rearrange("p a b c -> p (a b c)"), 0.0).then_inc(zeroed, 1)
            pool.memset(rows[:, :, :].rearrange("p a b -> p (a b)"), 0.0).then_inc(zeroed, 1)

            def pad_queries(q):
                for g, (c0, c1, n, t0) in enumerate(GROUPS):
                    w = (c1 - c0) * n
                    wait_apart(pool, phq_ready, 3 * q + g + 1, pool_waits)
                    for b in range(2):
                        half = slice(b * D, b * D + D)
                        ins = pool.tensor_scalar(phq_pad[half, b, t0:t0 + w], phq[half, t0:t0 + w], 1.0, 0.0,
                                                 ALU.mult, ALU.add)
                        ins.then_inc(phq_padded, 1)

            def scatter_rows(q):
                pool.wait_ge(slots_ready, q + 1)
                wait_apart(pool, xn2_in_rows, q + 1, pool_waits)
                for r in range(ROWS):
                    n = tokens_in(r // 2)
                    pool.indirect_dma_start(
                        slots, bass.IndirectOffsetOnAxis(ap=slot_idx[0:n, r:r + 1], axis=0), rows[0:n, r, :], None,
                        bounds_check=EXPERTS * CAPACITY - 1, oob_is_err=False).then_inc(rows_scattered, 16)

            pool.wait_ge(zeroed, ZEROED)
            pool.wait_ge(blank_written, 2 * 16 * EXPERTS)
            pool.sem_inc(rows_free, 1)
            with pool.Fori(0, PAIRS) as q:
                pad_queries(q)
                scatter_rows(q)
                pool.wait_ge(rows_scattered, (q + 1) * ROWS * 16)
                pool.wait_ge(h1_written, (q + 1) * 4 * 16)
                pool.sem_inc(rows_free, 1)

            pool.wait_ge(h1_written, PAIRS * 4 * 16)
            with pool.Fori(0, EXPERT_PAIRS * TURNS) as m:
                for u in range(SLOTS):
                    wait_apart(pool, y_ready, m * SLOTS + u + 1, pool_waits)
                    for v in range(2):
                        for n in range(STEP_TILES):
                            pool.indirect_dma_start(
                                out, bass.IndirectOffsetOnAxis(
                                    ap=y_token[u][:, v * STEP_TILES + n:v * STEP_TILES + n + 1], axis=0),
                                y_out[u][:, v, n, :], None,
                                bounds_check=TOKENS - 1, oob_is_err=False).then_inc(y_scattered[u], 16)
            for u in range(SLOTS):
                pool.wait_ge(y_scattered[u], EXPERT_PAIRS * TURNS * 2 * STEP_TILES * 16)

        @block.scalar
        def _(act):
            def copy_tok_hw(p, l):
                for h, (s0, s1, _, _) in enumerate(HALVES):
                    tok_filled(act, p, f"hw{l}", h)
                    act.activation(hw[:, s0:s1, :],
                                   bank[A[h]][0:NODE_CHUNK, 0:(s1 - s0) * P].rearrange("p (s n) -> p s n", n=P),
                                   ACT.Copy).then_inc(drained[A[h]], 1)

            def att_columns(q, use, dst, func, col):
                for g, (c0, c1, n, t0) in enumerate(GROUPS):
                    w = (c1 - c0) * n
                    att_filled(act, q, use, g)
                    b = {} if col is None else {"bias": bias[:, col:col + 1]}
                    act.activation(dst[:, t0:t0 + w], bank[X[g]][:, 0:w], func, **b).then_inc(drained[X[g]], 1)

            def sines(q, src, dst, first, ready):
                for g, (c0, c1, n, t0) in enumerate(GROUPS):
                    w = (c1 - c0) * n
                    act.wait_ge(folded, 6 * q + first + g + 1)
                    act.activation(dst[:, t0:t0 + w], src[:, t0:t0 + w], ACT.Sin, bias=cst("sin_bias"),
                                   scale=cst("sin_scale")).then_inc(ready, 1)

            def step(p, q):
                if q is not None:
                    act.activation(junk[:, :], cst("sin_bias"), ACT.Silu)
                    att_columns(q, "xnT", xnT, ACT.Copy, None)
                    att_columns(q, "q1", h1q, ACT.Tanh, 4)
                    att_columns(q, "k1", h1k, ACT.Tanh, 5)
                if p is not None:
                    copy_tok_hw(p, 0)
                if q is not None:
                    att_columns(q, "q2", tq, ACT.Tanh, 6)
                    att_columns(q, "k2", tk, ACT.Tanh, 7)
                if p is not None:
                    copy_tok_hw(p, 1)
                if q is not None:
                    sines(q, tk, phk, 3, phk_ready)
                    sines(q, tq, phq, 0, phq_ready)
                    for g, (c0, c1, n, _) in enumerate(GROUPS):
                        att_filled(act, q, "kT", g)
                        act.activation(phk_tok[0:n, c0:c1, :],
                                       bank[X[g]][0:n, 0:(c1 - c0) * P].rearrange("p (c n) -> p c n", n=P),
                                       ACT.Copy).then_inc(drained[X[g]], 1)
                if p is not None:
                    copy_tok_hw(p, 2)
                if q is not None:
                    act.wait_ge(xn2_ready, q + 1)
                    act.activation(rows[:, :, 0:D], xn2[:, :, :].rearrange("p c (b d) -> p (c b) d", d=D), ACT.Copy)\
                        .then_inc(xn2_in_rows, 1)
                    att_columns(q, "xn2T", xnT, ACT.Copy, None)
                    act.wait_ge(shifted_ready, q + 1)
                    act.activation(route[:, 1, :], route[:, 0, :], ACT.Exp).then_inc(exp_ready, 1)

            act.wait_ge(consts_loaded, 16)
            act.wait_ge(weights_loaded, WEIGHT_LOADS * 16)
            step(0, None)
            with act.Fori(1, PAIRS) as it:
                step(it, it - 1)
            step(None, PAIRS - 1)

            def copy_columns(step):
                act.wait_ge(filled[TB], number(step) + 1)
                act.activation(xT[step[2]], bank[TB][:, 0:STEP_COLS], ACT.Copy).then_inc(drained[TB], 1)

            def relu_hidden(step):
                for v, h in ((0, 0), (0, 1), (1, 0)):
                    b = HB[2 * v + h]
                    act.wait_ge(filled[b], BASE[b] + number(step) + 1)
                    act.activation(mid[step[2]][:, v, h, :], bank[b][:, 0:STEP_COLS], ACT.Relu,
                                   bias=b1_col[:, 2 * step[0] + v, h:h + 1]).then_inc(drained[b], 1)

            def expert_step(step):
                if later(step, 2):
                    copy_columns(later(step, 2))
                if later(step, 1):
                    relu_hidden(later(step, 1))

            act.wait_ge(expert_w_loaded, EXPERTS * 4 * 16)
            copy_columns((0, 0, 0))
            copy_columns((0, 0, 1))
            relu_hidden((0, 0, 0))
            for ep in range(EXPERT_PAIRS):
                with act.Fori(0, TURNS - 1) as i:
                    for u in range(SLOTS):
                        expert_step((ep, i, u))
                for u in range(SLOTS):
                    expert_step((ep, TURNS - 1, u))

        @block.tensor
        def _(pe):
            for half in range(2):
                pe.wait_ge(self_ready, half + 1)
                if half:
                    pe.wait_ge(counts_drained, NODE_CHUNKS)
                for s in range(NODE_CHUNKS):
                    pe.matmul(bank[s][0:NODE_CHUNK, 0:392], ident16[0:NODE_CHUNK, 0:NODE_CHUNK],
                              self_loop[half][:, s, :], start=True, stop=False)

                def count(i, u, last):
                    pe.wait_ge(hot_ready, (i + half * (EDGE_CHUNKS // EDGE_UNROLL)) * EDGE_UNROLL + u + 1)
                    for s in range(NODE_CHUNKS):
                        ins = pe.matmul(bank[s][0:NODE_CHUNK, 0:392],
                                        hot_src[0:EDGE_P, u, s * NODE_CHUNK:(s + 1) * NODE_CHUNK],
                                        hot_dst[0:EDGE_P, u, :], start=False, stop=last)
                    ins.then_inc(hot_used, 1)

                with pe.Fori(0, EDGE_CHUNKS // EDGE_UNROLL - 1) as i:
                    for u in range(EDGE_UNROLL):
                        count(i, u, False)
                for u in range(EDGE_UNROLL):
                    count(EDGE_CHUNKS // EDGE_UNROLL - 1, u, u == EDGE_UNROLL - 1)

            pe.wait_ge(counts_drained, 2 * NODE_CHUNKS)
            for h, (_, _, n0, w) in enumerate(HALVES):
                for s in range(NODE_CHUNKS):
                    ins = pe.matmul(bank[h][:, 0:w], ones[0:NODE_CHUNK, :], adj[:, s, n0:n0 + w],
                                    start=(s == 0), stop=(s == NODE_CHUNKS - 1))
                ins.then_inc(degree_filled, 1)
            pe.wait_ge(diag_ready, 1)
            for s in range(NODE_CHUNKS):
                h = 0 if s < 4 else 1
                at = (s - HALVES[h][0]) * NODE_CHUNK
                ins = pe.matmul(bank[h][0:P, at:at + NODE_CHUNK], ones[0:NODE_CHUNK, :], diag[:, s, :],
                                start=True, stop=True)
            ins.then_inc(dinv_filled, 1)

            pe.wait_ge(far_ready, 1)
            pe.matmul(bank[2][0:1, 0:1], far_sum[:, NODE_CHUNKS:NODE_CHUNKS + 1], ones[0:NODE_CHUNK, 0:1],
                      start=True, stop=True).then_inc(far_filled, 1)

            def embed(p):
                pe.wait_ge(image_loaded, (p + 1) * 12 * 16)
                for h in range(2):
                    tok_free(pe, p, "embed", h)
                    g0, g1 = ((0, 16), (16, 28))[h]
                    for m in range(4):
                        ins = pe.matmul(bank[A[h]][:, 0:(g1 - g0) * GRID], embed_w[:, m, :],
                                        image[:, g0:g1, 2 * m:SIDE:PATCH], start=(m == 0), stop=(m == 3))
                    ins.then_inc(filled[A[h]], 1)

            def node_products(p, use, w):
                for h, (s0, s1, _, _) in enumerate(HALVES):
                    tok_free(pe, p, use, h)
                    for s in range(s0, s1):
                        ins = pe.matmul(bank[A[h]][0:NODE_CHUNK, (s - s0) * P:(s - s0 + 1) * P],
                                        hT[:, s * NODE_CHUNK:(s + 1) * NODE_CHUNK], w, start=True, stop=True)
                    ins.then_inc(filled[A[h]], 1)

            def aggregate(p, l, h, banded):
                if h == 0:
                    for k in range(2):
                        tok_free(pe, p, f"agg{l}", k)
                d0, d1, n0, w = HALVES[h]
                if banded:
                    for d in range(d0, d1):
                        near = range(max(d - 1, 0), min(d + 2, NODE_CHUNKS))
                        for s in near:
                            ins = pe.matmul(bank[A[h]][:, (d - d0) * NODE_CHUNK:(d - d0 + 1) * NODE_CHUNK], hw[:, s, :],
                                            adj[:, s, d * NODE_CHUNK:(d + 1) * NODE_CHUNK],
                                            start=(s == near[0]), stop=(s == near[-1]))
                else:
                    for s in range(NODE_CHUNKS):
                        ins = pe.matmul(bank[A[h]][:, 0:w], hw[:, s, :], adj[:, s, n0:n0 + w],
                                        start=(s == 0), stop=(s == NODE_CHUNKS - 1))
                ins.then_inc(filled[A[h]], 1)

            def turn_tokens(q, use, src):
                for g, (c0, c1, n, _) in enumerate(GROUPS):
                    att_free(pe, q, use, g)
                    for c in range(c0, c1):
                        ins = pe.transpose(bank[X[g]][:, (c - c0) * n:(c - c0 + 1) * n], src(c, n),
                                           cst("ident")[0:n, 0:n])
                    ins.then_inc(filled[X[g]], 1)

            def project(q, use, w, src):
                for g, (c0, c1, n, t0) in enumerate(GROUPS):
                    cols = (c1 - c0) * n
                    att_free(pe, q, use, g)
                    ins = pe.matmul(bank[X[g]][:, 0:cols], w[:, :], src[:, t0:t0 + cols], start=True, stop=True)
                    ins.then_inc(filled[X[g]], 1)

            def values(q):
                for g, (c0, c1, n, _) in enumerate(GROUPS):
                    att_free(pe, q, "v", g)
                    for c in range(c0, c1):
                        t = first_token(c)
                        ins = pe.matmul(bank[X[g]][0:n, (c - c0) * P:(c - c0 + 1) * P], xnT[:, t:t + n], v_w[:, :],
                                        start=True, stop=True)
                    ins.then_inc(filled[X[g]], 1)

            def key_rows(q):
                for g, (c0, c1, n, _) in enumerate(GROUPS):
                    att_free(pe, q, "kT", g)
                    pe.wait_ge(phk_ready, 3 * q + g + 1)
                    for c in range(c0, c1):
                        t = first_token(c)
                        ins = pe.transpose(bank[X[g]][0:n, (c - c0) * P:(c - c0 + 1) * P], phk[:, t:t + n],
                                           cst("ident"))
                    ins.then_inc(filled[X[g]], 1)

            def key_values(q):
                for g, (c0, c1, n, _) in enumerate(GROUPS):
                    att_free(pe, q, "kv", g)
                    for c in range(c0, c1):
                        ins = pe.matmul(bank[X[g]][:, (c - c0) * P:(c - c0 + 1) * P], phk_tok[0:n, c, :],
                                        v_pad[0:n, c, 0:4:3, :], start=True, stop=True)
                    ins.then_inc(filled[X[g]], 1)

            def scores(q, f):
                score_free(pe, q, f)
                g = 0 if f < 2 else 1 if f < 4 else 2
                pe.wait_ge(phq_padded, 6 * q + 2 * g + 2)
                for j, c in enumerate(SCORE_FILLS[f]):
                    t, n = first_token(c), tokens_in(c)
                    ins = pe.matmul(score_view(f, n)[:, 2 * j:2 * j + 2, :], phk[:, t:t + n],
                                    phq_pad[:, :, t:t + n], start=True, stop=True)
                ins.then_inc(filled[S[f % 2]], 1)

            def retrieve(q, f):
                score_drained(pe, q, f)
                for j, c in enumerate(SCORE_FILLS[f]):
                    t, n = first_token(c), tokens_in(c)
                    g = [i for i, G in enumerate(GROUPS) if G[0] <= c < G[1]][0]
                    c0, c1 = GROUPS[g][0:2]
                    if c == c0:
                        att_free(pe, q, "out", g)
                    o = bank[X[g]][0:n, (c - c0) * P:(c - c0 + 1) * P]
                    if c:
                        pe.matmul(o, phq[:, t:t + n], state[:, c, :], start=True, stop=False)
                    for b in range(2):
                        ins = pe.matmul(o, masked[0:n, f % 3, 2 * j + b, 0:n], v_pad[0:n, c, 2 * b:2 * b + 2, :],
                                        start=(c == 0 and b == 0), stop=(b == 1))
                    if c == c1 - 1:
                        ins.then_inc(filled[X[g]], 1)

            def gates(q):
                score_free(pe, q, 6)
                for c in range(CHUNKS):
                    if c in (0, 4, 7):
                        att_drained(pe, q, "xn2T", (0, 4, 7).index(c))
                    t, n = first_token(c), tokens_in(c)
                    ins = pe.matmul(bank[S[0]][0:n, 16 * c:16 * c + 16], xnT[:, t:t + n], gate_w[:, :],
                                    start=True, stop=True)
                ins.then_inc(filled[S[0]], 1)

            def counts(q):
                score_free(pe, q, 7)
                pe.wait_ge(onehot_ready, q + 1)
                nodes, all_cols = NODE_CHUNKS * 2 * EXPERTS, ROWS * EXPERTS
                for k, lhs in enumerate((causal16, ones16)):
                    for n, lo, hi in ((NODE_CHUNK, 0, nodes), (TEXT_CHUNK, nodes, all_cols)):
                        ins = pe.matmul(bank[S[1]][:, k * all_cols + lo:k * all_cols + hi], lhs[0:n, :],
                                        onehot16[0:n, lo:hi], start=True, stop=True)
                ins.then_inc(filled[S[1]], 1)

            def step(p, q, banded):
                if p is not None:
                    embed(p)
                if q is not None:
                    pe.wait_ge(xn_ready, q + 1)
                    turn_tokens(q, "xnT", lambda c, n: xn[0:n, c, :, :].rearrange("p b d -> p (b d)"))
                    project(q, "q1", q1_w, xnT)
                    project(q, "k1", k1_w, xnT)
                if p is not None:
                    node_products(p, "hw0", gcn_w[:, 0, :])
                if q is not None:
                    values(q)
                    project(q, "q2", q2_w, h1q)
                    project(q, "k2", k2_w, h1k)
                if p is not None:
                    aggregate(p, 0, 0, banded)
                    aggregate(p, 0, 1, banded)
                    node_products(p, "hw1", gcn_w[:, 1, :])
                if q is not None:
                    key_rows(q)
                if p is not None:
                    aggregate(p, 1, 0, banded)
                    aggregate(p, 1, 1, banded)
                if q is not None:
                    key_values(q)
                    scores(q, 0)
                    scores(q, 1)
                if p is not None:
                    node_products(p, "hw2", gcn_w[:, 2, :])
                if q is not None:
                    for f in range(6):
                        retrieve(q, f)
                        if f + 2 < 6:
                            scores(q, f + 2)
                if p is not None:
                    aggregate(p, 2, 0, banded)
                    aggregate(p, 2, 1, banded)
                if q is not None:
                    pe.wait_ge(xn2_ready, q + 1)
                    turn_tokens(q, "xn2T", lambda c, n: xn2[0:n, c, :])
                    gates(q)
                if p is not None:
                    node_products(p, "out", out_w[:, :])
                if q is not None:
                    counts(q)

            pe.wait_ge(weights_loaded, WEIGHT_LOADS * 16)
            pe.wait_ge(zeroed, ZEROED)
            pe.wait_ge(adj_ready, 1)
            pe.wait_ge(far_known, 1)
            with pe.If(pe.value_load(far_edges[0:1, 0:1]) == 0):
                step(0, None, True)
                with pe.Fori(1, PAIRS) as it:
                    step(it, it - 1, True)
            with pe.Else():
                step(0, None, False)
                with pe.Fori(1, PAIRS) as it:
                    step(it, it - 1, False)
            step(None, PAIRS - 1, False)

            pe.wait_ge(expert_w_loaded, EXPERTS * 4 * 16)

            def turn_rows(step):
                n, u = number(step), step[2]
                pe.wait_ge(expert_xn_loaded[u], (step[1] + step[0] * TURNS + 1) * 2 * 16)
                pe.wait_ge(drained[TB], n + 1)
                for k in range(STEP_TILES):
                    ins = pe.transpose(bank[TB][:, k * TILE:(k + 1) * TILE],
                                       expert_xn[u][:, k, :, :].rearrange("p v d -> p (v d)"),
                                       cst("ident")[0:TILE, 0:TILE])
                ins.then_inc(filled[TB], 1)

            def up(step):
                n, u = number(step), step[2]
                pe.wait_ge(drained[TB], n + 2)
                for v in range(2):
                    for h in range(2):
                        b = HB[2 * v + h]
                        pe.wait_ge(drained[b], BASE[b] + n + 1)
                        pe.matmul(bank[b][:, 0:STEP_COLS], w1[:, step[0], v, h * P:(h + 1) * P], xT[u],
                                  start=True, stop=True).then_inc(filled[b], 1)

            def down(step):
                n, u = number(step), step[2]
                for v in range(2):
                    pe.wait_ge(drained[YB[v]], BASE[YB[v]] + n + 1)
                    for h in range(2):
                        b = HB[2 * v + h]
                        pe.wait_ge(drained[b], BASE[b] + n + 2)
                    for k in range(STEP_TILES):
                        for h in range(2):
                            ins = pe.matmul(bank[YB[v]][0:TILE, k * P:(k + 1) * P],
                                            mid[u][:, v, h, k * TILE:(k + 1) * TILE], w2[:, 2 * step[0] + v, h, :],
                                            start=(h == 0), stop=(h == 1))
                    ins.then_inc(filled[YB[v]], 1)

            def expert_step(step):
                if later(step, 2):
                    turn_rows(later(step, 2))
                if later(step, 1):
                    up(later(step, 1))
                down(step)

            turn_rows((0, 0, 0))
            turn_rows((0, 0, 1))
            up((0, 0, 0))
            for ep in range(EXPERT_PAIRS):
                with pe.Fori(0, TURNS - 1) as i:
                    for u in range(SLOTS):
                        expert_step((ep, i, u))
                for u in range(SLOTS):
                    expert_step((ep, TURNS - 1, u))

        @block.vector
        def _(dve):
            steps = Steps(dve, dve_steps)
            done, settle = steps.done, steps.settle
            TOTAL = [0]

            dve.wait_ge(consts_loaded, 16)
            done(dve.tensor_copy(nodes16, cst("nodes")))
            done(dve.tensor_copy(ident16[:, :], cst("ident")))
            done(dve.tensor_copy(causal16[:, :], cst("causal")))
            done(dve.memset(ones[:, :], 1.0))
            done(dve.memset(ones16[:, :], 1.0))
            done(dve.memset(base[:, :], 0.0))
            done(dve.memset(route[:, :, :].rearrange("p a b -> p (a b)"), 0.0))
            dve.wait_ge(edges_loaded, 16)
            done(dve.tensor_copy(edges_f[:, :, :], edges_i[:, :, :]))
            settle()
            for half in range(2):
                for s in range(NODE_CHUNKS):
                    ins = dve.tensor_scalar(self_loop[half][:, s, :], nodes16[0:NODE_CHUNK, 392 * half:392 * half + 392],
                                            cst("block_start", NODE_CHUNK)[:, s:s + 1], None, ALU.is_equal)
                    if s == NODE_CHUNKS - 1:
                        ins.then_inc(self_ready, 1)
            for half in range(2):
                def one_hot(i, u, first):
                    if not first:
                        dve.wait_ge(hot_used, (i - 1 + half * (EDGE_CHUNKS // EDGE_UNROLL)) * EDGE_UNROLL + u + 1)
                    dve.tensor_scalar(hot_src[0:EDGE_P, u, :], nodes16[0:EDGE_P, :],
                                      edges_f[:, 0, bass.ds(i * EDGE_UNROLL + u, 1)], None, ALU.is_equal)
                    dve.tensor_scalar(hot_dst[0:EDGE_P, u, :], nodes16[0:EDGE_P, 392 * half:392 * half + 392],
                                      edges_f[:, 1, bass.ds(i * EDGE_UNROLL + u, 1)], None, ALU.is_equal)\
                        .then_inc(hot_ready, 1)

                for u in range(EDGE_UNROLL):
                    one_hot(0, u, half == 0)
                with dve.Fori(1, EDGE_CHUNKS // EDGE_UNROLL) as i:
                    for u in range(EDGE_UNROLL):
                        one_hot(i, u, False)
                dve.wait_ge(hot_used, (half + 1) * EDGE_CHUNKS)
                for s in range(NODE_CHUNKS):
                    dve.tensor_copy(adj[:, s, 392 * half:392 * half + 392], bank[s][0:NODE_CHUNK, 0:392])\
                        .then_inc(counts_drained, 1)

            def rsqrt(y, v, vh, t):
                done(dve.tensor_scalar(vh, v, -0.5, None, ALU.mult))
                done(dve.tensor_scalar(y.bitcast(I32), v.bitcast(I32), -0.5, RSQRT_SEED, ALU.mult, ALU.add))
                settle()
                for _ in range(4):
                    done(dve.tensor_tensor(t, y, y, ALU.mult))
                    settle()
                    done(dve.tensor_tensor(t, t, vh, ALU.mult))
                    settle()
                    done(dve.scalar_tensor_tensor(y, t, 1.5, y, ALU.add, ALU.mult))
                    settle()

            for h, (s0, s1, _, _) in enumerate(HALVES):
                dve.wait_ge(degree_filled, h + 1)
                for s in range(s0, s1):
                    done(dve.tensor_tensor(diag[:, s, :], bank[h][0:NODE_CHUNK, (s - s0) * NODE_CHUNK:(s - s0 + 1) * NODE_CHUNK],
                                           cst("ident", NODE_CHUNK)[:, 0:NODE_CHUNK], ALU.mult))
            settle()
            deg, dinv = small[0:NODE_CHUNK, 0, 0:NODE_CHUNKS], small[0:NODE_CHUNK, 1, 0:NODE_CHUNKS]
            done(dve.tensor_reduce(deg, diag, AX.X, ALU.add))
            settle()
            rsqrt(dinv, deg, small[0:NODE_CHUNK, 2, 0:NODE_CHUNKS], small[0:NODE_CHUNK, 3, 0:NODE_CHUNKS])
            for s in range(NODE_CHUNKS):
                ins = dve.tensor_scalar(diag[:, s, :], cst("ident", NODE_CHUNK)[:, 0:NODE_CHUNK], dinv[:, s:s + 1], None,
                                        ALU.mult)
            ins.then_inc(diag_ready, 1)
            dve.wait_ge(dinv_filled, 1)
            dve.wait_ge(counts_drained, 2 * NODE_CHUNKS)
            for s in range(NODE_CHUNKS):
                lo, hi = max(s - 1, 0) * NODE_CHUNK, min(s + 2, NODE_CHUNKS) * NODE_CHUNK
                done(dve.tensor_reduce(far_sum[:, s:s + 1], adj[:, s, :], AX.X, ALU.add))
                done(dve.tensor_reduce(near_sum[:, s:s + 1], adj[:, s, lo:hi], AX.X, ALU.add))
            settle()
            done(dve.tensor_tensor(far_sum[:, 0:NODE_CHUNKS], far_sum[:, 0:NODE_CHUNKS], near_sum[:, :], ALU.subtract))
            settle()
            dve.tensor_reduce(far_sum[:, NODE_CHUNKS:NODE_CHUNKS + 1], far_sum[:, 0:NODE_CHUNKS], AX.X, ALU.add)\
                .then_inc(far_ready, 1)
            for s in range(NODE_CHUNKS):
                for h, (_, _, n0, w) in enumerate(HALVES):
                    ins = dve.scalar_tensor_tensor(adj[:, s, n0:n0 + w], adj[:, s, n0:n0 + w], dinv[:, s:s + 1],
                                                   bank[h][0:NODE_CHUNK, 0:w], ALU.mult, ALU.mult)
            ins.then_inc(adj_ready, 1)
            dve.wait_ge(far_filled, 1)
            dve.tensor_copy(far_edges[:, :], bank[2][0:1, 0:1]).then_inc(far_known, 1)
            dve.wait_ge(weights_loaded, WEIGHT_LOADS * 16)
            done(dve.tensor_scalar(pos_b[:, :], cst("position"), bias[:, 0:1], None, ALU.add))
            dve.wait_ge(zeroed, ZEROED)
            dve.wait_ge(adj_ready, 1)
            settle()
            for b in range(8):
                dve.sem_inc(drained[b], 1)

            def layer_norm(src, dst, ready, wait_text=None):
                for r in range(ROWS):
                    if r == 2 * NODE_CHUNKS and wait_text is not None:
                        dve.wait_ge(text_loaded, wait_text)
                    done(dve.bn_stats(stats[:, r, :], src[:, r, :]))
                settle()
                me, mo, se, so = (stats[:, :, k] for k in (1, 4, 2, 5))
                mean, dm, var, t, y, vh = (small[:, k, :] for k in range(6))
                done(dve.tensor_tensor(mean, me, mo, ALU.add))
                done(dve.tensor_tensor(dm, me, mo, ALU.subtract))
                done(dve.tensor_tensor(var, se, so, ALU.add))
                settle()
                done(dve.tensor_scalar(mean, mean, 0.5, None, ALU.mult))
                done(dve.tensor_tensor(dm, dm, dm, ALU.mult))
                done(dve.tensor_scalar(var, var, 1.0 / D, LN_EPS, ALU.mult, ALU.add))
                settle()
                wide = mean.unsqueeze(2).to_broadcast([P, ROWS, D])
                done(dve.tensor_tensor(dst, src, wide, ALU.subtract))
                done(dve.scalar_tensor_tensor(var, dm, 0.25, var, ALU.mult, ALU.add))
                settle()
                rsqrt(y, var, vh, t)
                dve.tensor_tensor(dst, dst, y.unsqueeze(2).to_broadcast([P, ROWS, D]), ALU.mult).then_inc(ready, 1)

            h0_rows = h0[:, :, :, :].rearrange("p c b d -> p (c b) d")
            xn_rows = xn[:, :, :, :].rearrange("p c b d -> p (c b) d")

            def store_embedding(p):
                for h, (_, _, n0, w) in enumerate(HALVES):
                    tok_filled(dve, p, "embed", h)
                    dve.tensor_tensor(hT[:, n0:n0 + w], bank[A[h]][:, 0:w], pos_b[:, n0:n0 + w], ALU.add)\
                        .then_inc(drained[A[h]], 1)

            def relu_nodes(p, l):
                for h, (_, _, n0, w) in enumerate(HALVES):
                    tok_filled(dve, p, f"agg{l}", h)
                    dve.tensor_scalar(hT[:, n0:n0 + w], bank[A[h]][:, 0:w], bias[:, l + 1:l + 2], 0.0,
                                      ALU.add, ALU.max).then_inc(drained[A[h]], 1)

            def store_nodes(p):
                for h, (s0, s1, _, _) in enumerate(HALVES):
                    tok_filled(dve, p, "out", h)
                    dve.tensor_tensor(h0[0:NODE_CHUNK, s0:s1, :, :],
                                      bank[A[h]][0:NODE_CHUNK, 0:(s1 - s0) * P]
                                      .rearrange("p (s b d) -> p s b d", b=2, d=D),
                                      out_b[0:NODE_CHUNK].unsqueeze(1).to_broadcast([NODE_CHUNK, s1 - s0, 2, D]),
                                      ALU.add).then_inc(drained[A[h]], 1)

            def norm_h0(p):
                for h in range(2):
                    dve.wait_ge(drained[A[h]], (p + 1) * len(TOK_USES) + 1)
                layer_norm(h0_rows, xn_rows, xn_ready, (p + 1) * 2 * 16)

            def store_values(q):
                for g, (c0, c1, n, _) in enumerate(GROUPS):
                    att_filled(dve, q, "v", g)
                    dve.tensor_tensor(v_pad[0:n, c0:c1, 0:4:3, :],
                                      bank[X[g]][0:n, 0:(c1 - c0) * P].rearrange("p (c b d) -> p c b d", b=2, d=D),
                                      v_b[0:n].unsqueeze(1).to_broadcast([n, c1 - c0, 2, D]),
                                      ALU.add).then_inc(drained[X[g]], 1)

            def fold(q, use, t):
                for g, (c0, c1, n, t0) in enumerate(GROUPS):
                    w = (c1 - c0) * n
                    att_drained(dve, q, use, g)
                    dve.scalar_tensor_tensor(t[:, t0:t0 + w], t[:, t0:t0 + w], cst("fold"), t[:, t0:t0 + w],
                                             ALU.mult, ALU.max).then_inc(folded, 1)

            def add_states(q):
                for g, (c0, c1, _, _) in enumerate(GROUPS):
                    att_filled(dve, q, "kv", g)
                    for c in range(c0, c1):
                        at = (c - c0) * P
                        if c < CHUNKS - 1:
                            for b in range(2):
                                half = slice(b * D, b * D + D)
                                new, part = state[half, c + 1, half], bank[X[g]][half, at + b * D:at + b * D + D]
                                if c == 0:
                                    done(dve.tensor_copy(new, part))
                                else:
                                    done(dve.tensor_tensor(new, part, state[half, c, half], ALU.add))
                            settle()
                    dve.tensor_copy(junk2[:, :], bank[X[g]][:, 0:1]).then_inc(drained[X[g]], 1)

            def mask_scores(q, f):
                score_filled(dve, q, f)
                n, k = tokens_in(SCORE_FILLS[f][0]), 2 * len(SCORE_FILLS[f])
                dve.tensor_tensor(masked[0:n, f % 3, 0:k, 0:n], score_view(f, n)[:, 0:k, :],
                                  cst("causal", n)[:, 0:n].unsqueeze(1).to_broadcast([n, k, n]), ALU.mult)\
                    .then_inc(drained[S[f % 2]], 1)

            def add_retrieved(q):
                dve.wait_ge(rows_free, q + 1)
                for g, (c0, c1, n, _) in enumerate(GROUPS):
                    att_filled(dve, q, "out", g)
                    tmp = xn[0:n, c0:c1, :, :].rearrange("p c b d -> p c (b d)")
                    done(dve.tensor_tensor(tmp, bank[X[g]][0:n, 0:(c1 - c0) * P].rearrange("p (c n) -> p c n", n=P),
                                           cst("rnorm", n)[:, c0:c1].unsqueeze(2).to_broadcast([n, c1 - c0, P]),
                                           ALU.mult))
                    settle()
                    dve.tensor_tensor(rows[0:n, 2 * c0:2 * c1, ROW_H:ROW_H + D], xn_rows[0:n, 2 * c0:2 * c1, :],
                                      h0_rows[0:n, 2 * c0:2 * c1, :], ALU.add).then_inc(drained[X[g]], 1)

            def norm_h1(q):
                for g in range(3):
                    att_drained(dve, q, "out", g)
                layer_norm(rows[:, :, ROW_H:ROW_H + D], xn2[:, :, :].rearrange("p c (b d) -> p (c b) d", d=D), xn2_ready)

            def by_expert(k):
                return route[:, k, :].rearrange("p (r e) -> p r e", e=EXPERTS)

            def wide(x):
                return x.unsqueeze(2).to_broadcast([P, ROWS, EXPERTS])

            def wide_e(x):
                return x.unsqueeze(1).to_broadcast([P, ROWS, EXPERTS])

            def shift_logits(q):
                score_filled(dve, q, 6)
                for n, c0, c1 in ((NODE_CHUNK, 0, NODE_CHUNKS), (TEXT_CHUNK, NODE_CHUNKS, CHUNKS)):
                    ins = dve.tensor_tensor(route[0:n, 2, 16 * c0:16 * c1].rearrange("p (c k) -> p c k", k=16),
                                            bank[S[0]][0:n, 16 * c0:16 * c1].rearrange("p (c k) -> p c k", k=16),
                                            gate_b[0:n].rearrange("p b e -> p (b e)").unsqueeze(1)
                                            .to_broadcast([n, c1 - c0, 16]), ALU.add)
                    if c0:
                        ins.then_inc(drained[S[0]], 1)
                    else:
                        done(ins)
                score_drained(dve, q, 6)
                settle()
                done(dve.tensor_reduce(small[:, 6, :], by_expert(2), AX.X, ALU.max))
                settle()
                dve.tensor_tensor(by_expert(0), by_expert(2), wide(small[:, 6, :]), ALU.subtract).then_inc(shifted_ready, 1)

            def choose(q):
                dve.wait_ge(exp_ready, q + 1)
                total, inv, prb, idx = (small[:, k, :] for k in (7, 8, 9, 10))
                done(dve.tensor_reduce(total, by_expert(1), AX.X, ALU.add))
                settle()
                done(dve.reciprocal(inv, total))
                settle()
                done(dve.tensor_tensor(by_expert(2), by_expert(1), wide(inv), ALU.mult))
                settle()
                done(dve.tensor_reduce(prb, by_expert(2), AX.X, ALU.max))
                settle()
                done(dve.tensor_tensor(by_expert(3), by_expert(2), wide(prb), ALU.is_ge))
                done(dve.tensor_copy(rows[:, :, ROW_PRB], prb))
                settle()
                done(dve.tensor_tensor(by_expert(3), by_expert(3), wide_e(cst("expert_less_8")), ALU.mult))
                settle()
                done(dve.tensor_reduce(idx, by_expert(3), AX.X, ALU.min))
                settle()
                done(dve.tensor_tensor(by_expert(4), wide_e(cst("expert_less_8")), wide(idx), ALU.is_equal))
                settle()
                dve.tensor_copy(onehot16[:, :], route[:, 4, :]).then_inc(onehot_ready, 1)

            def place(q):
                score_filled(dve, q, 7)
                n = ROWS * EXPERTS
                order = "p (c b e) -> p e b c"
                done(dve.tensor_copy(route[:, 5, :].rearrange("p (e b c) -> p e b c", e=EXPERTS, b=2),
                                     bank[S[1]][:, n:2 * n].rearrange(order, b=2, e=EXPERTS)))
                settle()
                done(dve.tensor_tensor_scan(route[:, 6, :], cst("carry"), route[:, 5, :], 0.0, ALU.mult, ALU.add))
                settle()
                done(dve.tensor_tensor(route[:, 5, :], route[:, 6, :], route[:, 5, :], ALU.subtract))
                settle()
                b3 = route[:, 5, :].rearrange("p (e r) -> p e r", e=EXPERTS)
                done(dve.tensor_tensor(b3, b3, base[:, :].unsqueeze(2).to_broadcast([P, EXPERTS, ROWS]), ALU.add))
                settle()
                done(dve.tensor_tensor(base[:, :], base[:, :],
                                       route[:, 6, :].rearrange("p (e r) -> p e r", e=EXPERTS)[:, :, ROWS - 1], ALU.add))
                dve.tensor_tensor(route[:, 7, :].rearrange("p (c b e) -> p c b e", b=2, e=EXPERTS)[:, :, 0, :],
                                  bank[S[1]][:, 0:n].rearrange("p (c b e) -> p c b e", b=2, e=EXPERTS)[:, :, 0, :],
                                  route[:, 5, :].rearrange("p (e b c) -> p c b e", e=EXPERTS, b=2)[:, :, 0, :], ALU.add)
                dve.tensor_tensor(route[:, 7, :].rearrange("p (c b e) -> p c b e", b=2, e=EXPERTS)[:, :, 1, :],
                                  bank[S[1]][:, 0:n].rearrange("p (c b e) -> p c b e", b=2, e=EXPERTS)[:, :, 1, :],
                                  route[:, 5, :].rearrange("p (e b c) -> p c b e", e=EXPERTS, b=2)[:, :, 1, :], ALU.add)\
                    .then_inc(drained[S[1]], 1)
                score_drained(dve, q, 7)
                done(dve.tensor_scalar(route[:, 6, :], route[:, 7, :], float(CAPACITY), float(NOWHERE), ALU.is_gt, ALU.mult))
                done(dve.tensor_tensor(by_expert(7), by_expert(7), wide_e(cst("slot_base")), ALU.add))
                settle()
                done(dve.tensor_tensor(route[:, 7, :], route[:, 7, :], route[:, 6, :], ALU.add))
                settle()
                done(dve.tensor_tensor(route[:, 7, :], route[:, 7, :], route[:, 4, :], ALU.mult))
                settle()
                done(dve.tensor_reduce(small[:, 11, :], by_expert(7), AX.X, ALU.add))
                done(dve.tensor_copy(rows[:, :, ROW_TOK].bitcast(I32), cst("token")))
                settle()
                done(dve.tensor_scalar(cst("token"), cst("token"), float(2 * L), None, ALU.add))
                dve.tensor_copy(slot_idx[:, :], small[:, 11, :]).then_inc(slots_ready, 1)
                settle()

            def step(p, q):
                if p is not None:
                    store_embedding(p)
                if q is not None:
                    store_values(q)
                    fold(q, "q2", tq)
                    fold(q, "k2", tk)
                if p is not None:
                    relu_nodes(p, 0)
                    relu_nodes(p, 1)
                if q is not None:
                    add_states(q)
                    for f in range(6):
                        mask_scores(q, f)
                    add_retrieved(q)
                    norm_h1(q)
                if p is not None:
                    relu_nodes(p, 2)
                if q is not None:
                    shift_logits(q)
                    choose(q)
                if p is not None:
                    store_nodes(p)
                if q is not None:
                    place(q)
                if p is not None:
                    norm_h0(p)

            step(0, None)
            total = steps.n
            with dve.Fori(1, PAIRS) as it:
                steps.begin((it - 1) * LOOP_STEPS + total)
                step(it, it - 1)
                assert steps.n == LOOP_STEPS, steps.n
            steps.begin(total + (PAIRS - 1) * LOOP_STEPS)
            step(None, PAIRS - 1)
            total = steps.base + steps.n

            def relu_hidden(step):
                b = HB[3]
                dve.wait_ge(filled[b], BASE[b] + number(step) + 1)
                dve.tensor_scalar(mid[step[2]][:, 1, 1, :], bank[b][:, 0:STEP_COLS],
                                  b1_col[:, 2 * step[0] + 1, 1:2], 0.0, ALU.add, ALU.max).then_inc(drained[b], 1)

            def expert_step(step):
                if later(step, 1):
                    relu_hidden(later(step, 1))
                ep, i, u = step
                m = i + ep * TURNS
                n = number(step)
                y, low, high, fin = y_work
                for v in range(2):
                    e = 2 * ep + v
                    dve.wait_ge(filled[YB[v]], BASE[YB[v]] + n + 1)
                    dve.tensor_tensor(y[:, v], bank[YB[v]][0:TILE, 0:STEP_TILES * P]
                                      .rearrange("p (k n) -> p k n", n=P)[:, :, 0:D],
                                      b2_row[0:TILE, e, :].unsqueeze(1).to_broadcast([TILE, STEP_TILES, D]),
                                      ALU.add).then_inc(drained[YB[v]], 1)
                for v in range(2):
                    dve.wait_ge(drained[YB[v]], BASE[YB[v]] + n + 2)
                er = expert_rows[u][:, :, :, :].rearrange("p v k r -> p (v k) r")
                yf, lf, hf, ff = (t.rearrange("p v k d -> p (v k) d") for t in (y, low, high, fin))
                dve.wait_ge(rows_loaded[u], (m + 1) * 2 * 16)
                done(dve.tensor_tensor(yf, yf, er[:, :, ROW_PRB - D:ROW_PRB + 1 - D].to_broadcast([TILE, 6, D]), ALU.mult))
                settle()
                done(dve.tensor_scalar(lf, yf, 0.0, -1e4, ALU.min, ALU.max))
                done(dve.tensor_scalar(hf, yf, 0.0, 1e4, ALU.max, ALU.min))
                done(dve.tensor_scalar(ff.bitcast(I32), yf, 0.0, 0.0, ALU.mult, ALU.is_equal))
                settle()
                done(dve.tensor_tensor(lf, lf, hf, ALU.add))
                wait_apart(dve, dve_steps, steps.base + steps.n, dve_waits)
                done(dve.copy_predicated(lf, ff.bitcast(I32), yf))
                settle()
                if not (isinstance(m, int) and m == 0):
                    dve.wait_ge(y_scattered[u], m * 2 * STEP_TILES * 16)
                done(dve.tensor_copy(y_token[u][:, :], er[:, :, ROW_TOK - D].bitcast(I32)))
                settle()
                dve.tensor_tensor(y_out[u].rearrange("p v k d -> p (v k) d"), lf, er[:, :, 0:D], ALU.add)\
                    .then_inc(y_ready, 1)

            dve.wait_ge(expert_w_loaded, EXPERTS * 4 * 16)
            relu_hidden((0, 0, 0))
            for ep in range(EXPERT_PAIRS):
                first = 1 if ep == 0 else 0
                steps.begin(total)
                for u in range(SLOTS * first):
                    expert_step((0, 0, u))
                total += steps.n
                with dve.Fori(first, TURNS - 1) as i:
                    steps.begin((i - first) * FFN_LOOP_STEPS + total)
                    for u in range(SLOTS):
                        expert_step((ep, i, u))
                    assert steps.n == FFN_LOOP_STEPS, steps.n
                total += (TURNS - 1 - first) * FFN_LOOP_STEPS
                steps.begin(total)
                for u in range(SLOTS):
                    expert_step((ep, TURNS - 1, u))
                total += steps.n


def constants():
    import numpy as np

    c = np.zeros((P, CONST_COLS), np.float32)

    def put(name, value):
        c[:, CONST[name][0]:CONST[name][1]] = value

    p = np.arange(P)
    put("ident", np.eye(P))
    put("causal", p[:, None] <= p[None, :])
    pos = np.arange(NODES, dtype=np.float32)[:, None]
    div = np.exp(np.arange(0, D, 2, dtype=np.float32) * np.float32(-np.log(10000.0) / D))
    pe = np.zeros((NODES, D), np.float32)
    pe[:, 0::2], pe[:, 1::2] = np.sin(pos * div), np.cos(pos * div)
    put("position", np.concatenate([pe.T, pe.T]))
    put("nodes", np.arange(NODES)[None])
    first = np.array([first_token(k) for k in range(CHUNKS)])
    put("rnorm", 1 / np.sqrt((first[None] + p[:, None] + 1.0) * PHASES))
    put("expert_less_8", np.arange(EXPERTS)[None] - 8)
    put("slot_base", np.arange(EXPERTS)[None] * CAPACITY - 1)
    put("carry", (np.arange(EXPERTS * ROWS) % ROWS != 0)[None])
    put("token", np.repeat(first, 2)[None] + np.tile([0, L], CHUNKS)[None] + p[:, None])
    cosine = (p % D < PHASES)
    put("fold", np.where(cosine, -1, 1)[:, None])
    put("sin_scale", np.where(cosine, -PI, PI)[:, None])
    put("sin_bias", np.where(cosine, PI / 2, 0)[:, None])
    put("block_start", p[:, None] + np.arange(NODE_CHUNKS)[None] * NODE_CHUNK)
    return c


def kernel(**inputs):
    import numpy as np
    import concourse.bacc as bacc
    from concourse.bass_utils import run_bass_kernel_spmd

    short = {"x": "x", "txt": "txt", "L0_tok_edge_index": "edge_index"}
    for n in ("W_embed", "b_embed", "W_gcn", "b_gcn", "W_out", "b_out"):
        short["L0_tok_" + n] = n
    for n in ("kb1", "kb2", "qb1", "qb2", "vb"):
        short["L0_attn_" + n] = n
    for n in ("gate_w", "gate_b", "w1", "b1", "w2", "b2"):
        short["L0_ffn_" + n] = n
    arrays = {v: np.ascontiguousarray(inputs[k]) for k, v in short.items()}
    for n in ("kw1", "kw2", "qw1", "qw2", "vw"):
        arrays[n + "T"] = np.ascontiguousarray(np.transpose(inputs["L0_attn_" + n]))
    arrays["constants"] = constants()

    nc = bacc.Bacc("TRN2", target_bir_lowering=False, num_devices=1)
    d = {n: nc.dram_tensor("in_" + n, a.shape, mybir.dt.from_np(a.dtype), kind="ExternalInput").ap()
         for n, a in arrays.items()}
    d["out"] = nc.dram_tensor("out_rows", (BATCH, L, D), F32, kind="ExternalOutput").ap()
    build(nc, d)
    r = run_bass_kernel_spmd(nc, [{"in_" + n: a for n, a in arrays.items()}], core_ids=[0])
    return r.results[0]["out_rows"]
```

```python
import concourse.bass as bass
from concourse import mybir
from contextlib import ExitStack

F32 = mybir.dt.float32
F16 = mybir.dt.float16
I32 = mybir.dt.int32
ALU = mybir.AluOpType
ACT = mybir.ActivationFunctionType
AX = mybir.AxisListType

P = 128
BATCH = 16
PAIRS = BATCH // 2
D = 64
GRID = 28
PATCH = 8
CHANNELS = 3
SIDE = GRID * PATCH
NODES = GRID * GRID
TEXT = 512
L = NODES + TEXT
EDGES = 2 * 2 * GRID * (GRID - 1)
LAYERS = 3
PHASES = 32
EXPERTS = 8
HIDDEN = 256
TOKENS = BATCH * L
CAPACITY = -(-5 * TOKENS // (4 * EXPERTS))
LN_EPS = 1e-5
RSQRT_SEED = float(0x5F3759DF)
PI = 3.141592653589793

NODE_CHUNK, NODE_CHUNKS = 112, NODES // 112
TEXT_CHUNK, TEXT_CHUNKS = 128, TEXT // 128
CHUNKS = NODE_CHUNKS + TEXT_CHUNKS
ROWS = 2 * CHUNKS
GROUPS = [(0, 4, 112, 0), (4, 7, 112, 448), (7, 11, 128, 784)]
SCORE_FILLS = [(0, 1), (2, 3), (4, 5), (6,), (7, 8), (9, 10)]
EDGE_P = 126
EDGE_CHUNKS = EDGES // EDGE_P
EDGE_UNROLL = 4
EDGE_TURNS = EDGE_CHUNKS // EDGE_UNROLL
HALF_NODES = NODES // 2

ROW = 132
ROW_H, ROW_PRB, ROW_TOK = D, 2 * D, 2 * D + 1
NOWHERE = 1 << 20

TILE = 120
TILES = CAPACITY // TILE
STEP_TILES = 3
STEPS = TILES // STEP_TILES
STEP_COLS = STEP_TILES * TILE
EXPERT_PAIRS = EXPERTS // 2
BLANK_ROWS = 9
SLOTS = 3
TURNS = STEPS // SLOTS

TOK_USES = ["embed", "hw0", "agg0", "hw1", "agg1", "hw2", "agg2", "out"]
ATT_USES = ["xnT", "k1", "q1", "v", "k2", "q2", "xn2T", "kT", "kv", "out"]

EMBED_LOADS = 2 * 2 * CHANNELS
TOK_LOADS = 2 * 5
ATT_LOADS = 2 * (3 + 4 + 1 + 2 + 4 + 2)
ZEROED = 7
BASE = {0: 8 * PAIRS, 1: 8 * PAIRS, 2: 10 * PAIRS, 3: 10 * PAIRS, 4: 10 * PAIRS, 5: 3 * PAIRS, 7: 2 * PAIRS}
LOOP_STEPS = 125
FFN_LOOP_STEPS = 21

_widths = [("ident", P), ("causal", P), ("position", NODES), ("nodes", NODES), ("rnorm", CHUNKS),
           ("expert_less_8", EXPERTS), ("slot_base", EXPERTS), ("carry", EXPERTS * ROWS), ("token", ROWS),
           ("fold", 1), ("sin_scale", 1), ("sin_bias", 1)]
CONST = {}
_at = 0
for _n, _w in _widths:
    CONST[_n] = (_at, _at + _w)
    _at += _w
CONST_COLS = _at


def first_token(chunk):
    return chunk * NODE_CHUNK if chunk < NODE_CHUNKS else NODES + (chunk - NODE_CHUNKS) * TEXT_CHUNK


def tokens_in(chunk):
    return NODE_CHUNK if chunk < NODE_CHUNKS else TEXT_CHUNK


def later(step, k):
    ep, i, u = step
    i, u = i + (u + k) // SLOTS, (u + k) % SLOTS
    if isinstance(i, int) and i >= TURNS:
        ep, i = ep + 1, i - TURNS
    return (ep, i, u) if ep < EXPERT_PAIRS else None


def number(step):
    ep, i, u = step
    return (i + ep * TURNS) * SLOTS + u


def wait_apart(eng, sem, value, waits):
    eng.wait_ge(sem, value)
    eng.sem_inc(waits, 1)


class Steps:

    def __init__(self, eng, sem):
        self.eng, self.sem, self.base, self.n = eng, sem, 0, 0

    def done(self, ins):
        self.n += 1
        ins.then_inc(self.sem, 1)

    def settle(self):
        self.eng.wait_ge(self.sem, self.base + self.n)

    def begin(self, base):
        self.base, self.n = base, 0


def build(nc, d):
    ctx = ExitStack()
    with ctx:
        def sb(name, shape, dt=F32):
            return ctx.enter_context(nc.sbuf_tensor("sb_" + name, shape, dt))

        def sem(name):
            return ctx.enter_context(nc.semaphore(name))

        slots = nc.dram_tensor("expert_slots", [EXPERTS * CAPACITY, ROW], F32, kind="Internal").ap()
        out = d["out"].rearrange("b l d -> (b l) d")

        const = sb("const", [P, CONST_COLS])

        def cst(name, p=P):
            return const[0:p, CONST[name][0]:CONST[name][1]]

        causal16 = sb("causal16", [P, P], F16)
        ones16 = sb("ones16", [P, P], F16)
        ones = sb("ones", [P, P])
        embed_w = sb("embed_w", [96, 4, P])
        gcn_w = sb("gcn_w", [P, LAYERS, P])
        out_w = sb("out_w", [P, P])
        q1_w, k1_w, v_w = sb("q1_w", [P, P]), sb("k1_w", [P, P]), sb("v_w", [P, P])
        q2_w, k2_w = sb("q2_w", [P, P]), sb("k2_w", [P, P])
        gate_w = sb("gate_w", [P, 2 * EXPERTS])
        bias = sb("bias", [P, 8])
        b1_col = sb("b1_col", [P, EXPERTS, 2])
        out_b, v_b = sb("out_b", [P, 2, D]), sb("v_b", [P, 2, D])
        gate_b = sb("gate_b", [P, 2, EXPERTS])
        b2_row = sb("b2_row", [P, EXPERTS, D])
        w1 = sb("w1", [P, EXPERT_PAIRS, 2, HIDDEN])
        w2 = sb("w2", [P, EXPERTS, 2, P])
        adj = sb("adj", [NODE_CHUNK, NODE_CHUNKS, NODES])
        pos_b = sb("pos_b", [P, NODES])

        image = sb("image", [96, GRID, SIDE])
        hT = sb("hT", [P, NODES])
        hw = sb("hw", [NODE_CHUNK, NODE_CHUNKS, P])
        h0 = sb("h0", [P, CHUNKS, 2, D])
        xn = sb("xn", [P, CHUNKS, 2, D])
        xnT = sb("xnT", [P, L])
        h1q, h1k = sb("h1q", [P, L]), sb("h1k", [P, L])
        tq, tk = sb("tq", [P, L]), sb("tk", [P, L])
        phq, phk = sb("phq", [P, L]), sb("phk", [P, L])
        phq_pad = sb("phq_pad", [P, 2, L])
        phk_tok = sb("phk_tok", [P, CHUNKS, P])
        xn2 = xn[:, :, :, :].rearrange("p c b d -> p c (b d)")
        v_pad = sb("v_pad", [P, CHUNKS, 4, D])
        state = sb("state", [P, CHUNKS, P])
        h1 = sb("h1", [P, ROWS, D])
        masked = sb("masked", [P, 3, 4, P])
        rows = sb("rows", [P, ROWS, ROW])
        small = sb("small", [P, 24, ROWS])
        stats = sb("stats", [P, ROWS, 6])
        route = sb("route", [P, 8, ROWS * EXPERTS])
        onehot16 = sb("onehot16", [P, ROWS * EXPERTS], F16)
        base = sb("base", [P, EXPERTS])
        slot_idx = sb("slot_idx", [P, ROWS], I32)
        far_edges = sb("far_edges", [1, 1], I32)
        edge_block = sb("edge_block", [EDGE_P, 2, EDGE_CHUNKS])
        far_sum = sb("far_sum", [EDGE_P, 1])
        junk = [sb(f"junk{i}", [P, 1]) for i in range(2)]

        nodes16 = hT[:, 0:NODES // 2].bitcast(F16)
        ident16 = sb("ident16", [P, P], F16)
        zero16 = sb("zero16", [P, 2], F16)
        edges_i = sb("edges_i", [EDGE_P, 2, EDGE_CHUNKS], I32)
        edges_f = sb("edges_f", [EDGE_P, 2, EDGE_CHUNKS])
        hot_src = phq_pad[:, :, :].rearrange("p a b -> p (a b)")[:, 0:EDGE_UNROLL * NODES // 2].bitcast(F16)\
            .rearrange("p (u n) -> p u n", u=EDGE_UNROLL)
        hot_dst = v_pad[:, :, :, :].rearrange("p a b c -> p (a b c)")[:, 0:EDGE_UNROLL * NODES // 2].bitcast(F16)\
            .rearrange("p (u n) -> p u n", u=EDGE_UNROLL)
        diag = phk_tok[0:NODE_CHUNK, 0:NODE_CHUNKS, 0:NODE_CHUNK]
        blank = phk[0:TILE, 0:BLANK_ROWS * ROW]

        def flat(t, p, n):
            names = "abc"[0:len(t.shape) - 1]
            v = t[:, :] if len(names) == 1 else t[tuple([slice(None)] * len(t.shape))].rearrange(
                f"p {' '.join(names)} -> p ({' '.join(names)})")
            return v[0:p, 0:n]

        expert_xn = [sb(f"expert_xn{u}", [TILE, STEP_TILES, 2, D]) for u in range(SLOTS)]
        expert_rows = [flat(state, TILE, CHUNKS * P)[:, 408 * u:408 * u + 408]
                       .rearrange("p (v n r) -> p v n r", v=2, r=ROW - D) for u in range(SLOTS)]
        xT = [t[:, 0:STEP_COLS] for t in (xnT, h1q, h1k)]
        mid = [flat(t, P, 4 * STEP_COLS).rearrange("p (v h n) -> p v h n", v=2, h=2) for t in (phq_pad, v_pad, masked)]
        y_work = [flat(t, TILE, 2 * STEP_TILES * D).rearrange("p (v n d) -> p v n d", v=2, d=D)
                  for t in (tq, tk, phq, phk)]
        y_out = [flat(h0, TILE, CHUNKS * P)[:, 384 * u:384 * u + 384].rearrange("p (v n d) -> p v n d", v=2, d=D)
                 for u in range(SLOTS)]
        y_token = [sb(f"y_token{u}", [TILE, 2 * STEP_TILES], I32) for u in range(SLOTS)]
        TB, HB, YB = 7, [0, 1, 2, 3], [4, 5]

        bank = [ctx.enter_context(nc.psum_tensor(f"bank{i}", [P, 512], F32)) for i in range(8)]
        A, X, S, R = [0, 1], [2, 3, 4], [5, 6], 7

        filled = [sem(f"filled_bank{i}") for i in range(8)]
        drained = [sem(f"drained_bank{i}") for i in range(8)]
        consts_loaded = sem("consts_loaded")
        embed_w_loaded, tok_w_loaded, att_w_loaded = sem("embed_w_loaded"), sem("tok_w_loaded"), sem("att_w_loaded")
        expert_w_loaded = sem("expert_w_loaded")
        edges_loaded = sem("edges_loaded")
        image_loaded = sem("image_loaded")
        text_loaded = sem("text_loaded")
        zeroed = sem("zeroed")
        blank_ready = sem("blank_ready")
        blank_written = sem("blank_written")
        dve_steps = sem("dve_steps")
        hot_ready = sem("hot_ready")
        hot_used = sem("hot_used")
        setup_steps = sem("setup_steps")
        counts_filled, counts_drained = sem("counts_filled"), sem("counts_drained")
        degree_filled = sem("degree_filled")
        diag_ready = sem("diag_ready")
        dinv_filled = sem("dinv_filled")
        far_ready, far_filled, far_known = sem("far_ready"), sem("far_filled"), sem("far_known")
        adj_ready = sem("adj_ready")
        xn_ready = sem("xn_ready")
        folded = sem("folded")
        phq_ready = sem("phq_ready")
        phk_ready = sem("phk_ready")
        phq_padded = sem("phq_padded")
        xn2_ready = sem("xn2_ready")
        h0_kept = sem("h0_kept")
        h1_in_rows, norm_in_rows = sem("h1_in_rows"), sem("norm_in_rows")
        shifted_ready = sem("shifted_ready")
        exp_ready = sem("exp_ready")
        onehot_ready = sem("onehot_ready")
        slots_ready = sem("slots_ready")
        rows_scattered = sem("rows_scattered")
        h1_written = sem("h1_written")
        rows_free = sem("rows_free")
        expert_xn_loaded = [sem(f"expert_xn_loaded{u}") for u in range(SLOTS)]
        rows_loaded = [sem(f"rows_loaded{u}") for u in range(SLOTS)]
        y_ready = sem("y_ready")
        y_scattered = [sem(f"y_scattered{u}") for u in range(SLOTS)]
        pool_steps = sem("pool_steps")
        pool_waits, dve_waits = sem("pool_waits"), sem("dve_waits")

        block = ctx.enter_context(nc.Block())

        def att_fill(q, use):
            if use == "xn2T":
                if isinstance(q, int) and q == PAIRS - 1:
                    return PAIRS * len(ATT_USES) - 1
                return (q + 1) * len(ATT_USES) + ATT_USES.index(use) - 1
            at = ATT_USES.index(use)
            if at > ATT_USES.index("xn2T") or not (isinstance(q, int) and q == 0):
                at -= 1
            return q * len(ATT_USES) + at

        def att_filled(eng, q, use, g):
            eng.wait_ge(filled[X[g]], att_fill(q, use) + 1)

        def att_free(eng, q, use, g):
            eng.wait_ge(drained[X[g]], att_fill(q, use) + 1)

        def att_drained(eng, q, use, g):
            eng.wait_ge(drained[X[g]], att_fill(q, use) + 2)

        def tok_filled(eng, p, use, h):
            eng.wait_ge(filled[A[h]], p * len(TOK_USES) + TOK_USES.index(use) + 1)

        def tok_free(eng, p, use, h):
            eng.wait_ge(drained[A[h]], p * len(TOK_USES) + TOK_USES.index(use) + 1)

        def score_filled(eng, q, f):
            eng.wait_ge(filled[S[f % 2]], q * 3 + f // 2 + 1)

        def score_free(eng, q, f):
            eng.wait_ge(drained[S[f % 2]], q * 3 + f // 2 + 1)

        def score_drained(eng, q, f):
            eng.wait_ge(drained[S[f % 2]], q * 3 + f // 2 + 2)

        def route_filled(eng, r, use):
            eng.wait_ge(filled[R], r * 2 + use + 1)

        def route_free(eng, r, use):
            eng.wait_ge(drained[R], r * 2 + use + 1)

        def route_drained(eng, r, use):
            eng.wait_ge(drained[R], r * 2 + use + 2)

        def score_view(f, n):
            return bank[S[f % 2]][0:n, :].rearrange("p (k n) -> p k n", n=P)[:, :, 0:n]

        NEAR_WINDOWS = [(max(s - 1, 0) * NODE_CHUNK, min(s + 2, NODE_CHUNKS) * NODE_CHUNK) for s in range(NODE_CHUNKS)]
        HALVES = [(0, 4, 0, 448), (4, 7, 448, 336)]

        @block.sync
        def _(sp):
            sp.dma_start(const[:, :], d["constants"]).then_inc(consts_loaded, 16)
            sp.dma_start(edges_i[:, :, :], d["edge_index"].rearrange("t (p c) -> p t c", p=EDGE_P))\
                .then_inc(edges_loaded, 16)
            def load_image(p):
                for s in range(2):
                    for b in range(2):
                        for c in range(CHANNELS):
                            row = 48 * s + 24 * b + 8 * c
                            src = d["x"][bass.ds(p * 2 + b, 1), c].rearrange("o (g i) w -> i (o g) w", i=PATCH)
                            sp.dma_start(image[row:row + PATCH, :, 0:SIDE - s], src[:, :, s:SIDE])\
                                .then_inc(image_loaded, 16)

            def load_text(p):
                for b in range(2):
                    src = d["txt"][bass.ds(p * 2 + b, 1)].rearrange("o (t p) d -> p (o t) d", p=TEXT_CHUNK)
                    sp.dma_start(h0[:, NODE_CHUNKS:, b, :], src).then_inc(text_loaded, 16)

            def store_h1(q):
                for b in range(2):
                    dst = d["out"][bass.ds(q * 2 + b, 1)]
                    src = rows[:, :, ROW_H:ROW_H + D].rearrange("p (c b) d -> p c b d", b=2)[:, :, b, :]
                    sp.dma_start(dst[:, 0:NODES].rearrange("o (c p) d -> p (o c) d", p=NODE_CHUNK),
                                 src[0:NODE_CHUNK, 0:NODE_CHUNKS]).then_inc(h1_written, 16)
                    sp.dma_start(dst[:, NODES:L].rearrange("o (c p) d -> p (o c) d", p=TEXT_CHUNK),
                                 src[:, NODE_CHUNKS:]).then_inc(h1_written, 16)

            sp.wait_ge(zeroed, 1)
            w = d["W_embed"].rearrange("(c i m s) h -> s c i m h", c=CHANNELS, i=PATCH, s=2)
            for s in range(2):
                for b in range(2):
                    for c in range(CHANNELS):
                        row = 48 * s + 24 * b + 8 * c
                        sp.dma_start(embed_w[row:row + PATCH, :, b * D:b * D + D], w[s, c]).then_inc(embed_w_loaded, 16)
            load_image(0)
            halves = [slice(b * D, b * D + D) for b in range(2)]
            for b, half in enumerate(halves):
                sp.dma_start(bias[half, 0:1], d["b_embed"].unsqueeze(1)).then_inc(tok_w_loaded, 16)
                sp.dma_start(gcn_w[half, :, half], d["W_gcn"].rearrange("l i o -> i l o")).then_inc(tok_w_loaded, 16)
                sp.dma_start(bias[half, 1:1 + LAYERS], d["b_gcn"].rearrange("l f -> f l"),
                             allow_slow_non_contiguous=True).then_inc(tok_w_loaded, 16)
                sp.dma_start(out_w[half, half], d["W_out"]).then_inc(tok_w_loaded, 16)
                sp.dma_start(out_b[:, b, :], d["b_out"].partition_broadcast(P)).then_inc(tok_w_loaded, 16)
            for b, half in enumerate(halves):
                for tile, name in ((q1_w, "qw1T"), (k1_w, "kw1T"), (v_w, "vwT")):
                    sp.dma_start(tile[half, half], d[name]).then_inc(att_w_loaded, 16)
                for tile, name in ((q2_w, "qw2T"), (k2_w, "kw2T")):
                    for r in range(2):
                        at = b * D + r * PHASES
                        sp.dma_start(tile[half, at:at + PHASES], d[name]).then_inc(att_w_loaded, 16)
                sp.dma_start(gate_w[half, b * EXPERTS:(b + 1) * EXPERTS], d["gate_w"]).then_inc(att_w_loaded, 16)
                for i, name in ((4, "qb1"), (5, "kb1")):
                    sp.dma_start(bias[half, i:i + 1], d[name].unsqueeze(1)).then_inc(att_w_loaded, 16)
                for i, name in ((6, "qb2"), (7, "kb2")):
                    for r in range(2):
                        at = b * D + r * PHASES
                        sp.dma_start(bias[at:at + PHASES, i:i + 1], d[name].unsqueeze(1)).then_inc(att_w_loaded, 16)
                for tile, name in ((v_b, "vb"), (gate_b, "gate_b")):
                    sp.dma_start(tile[:, b, :], d[name].partition_broadcast(P)).then_inc(att_w_loaded, 16)
            sp.wait_ge(zeroed, 2)
            load_text(0)
            sp.wait_ge(filled[A[1]], 1)
            load_image(1)
            sp.wait_ge(zeroed, 3)
            for e in range(EXPERTS):
                at = D * (e % 2)
                sp.dma_start(w1[at:at + D, e // 2, e % 2, :], d["w1"][e]).then_inc(expert_w_loaded, 16)
                sp.dma_start(w2[:, e, :, 0:D], d["w2"][e].rearrange("(h f) d -> f h d", h=2))\
                    .then_inc(expert_w_loaded, 16)
                sp.dma_start(b1_col[:, e, :], d["b1"][e].rearrange("(h f) -> f h", h=2),
                             allow_slow_non_contiguous=True).then_inc(expert_w_loaded, 16)
                sp.dma_start(b2_row[:, e, :], d["b2"][e].partition_broadcast(P)).then_inc(expert_w_loaded, 16)

            def turn(p, r):
                if not (isinstance(p, int) and p == PAIRS - 1):
                    sp.wait_ge(filled[A[1]], p * len(TOK_USES) + 1)
                    load_image(p + 1)
                sp.wait_ge(h0_kept, p)
                load_text(p)
                if r is not None:
                    sp.wait_ge(slots_ready, r + 1)
                    sp.wait_ge(h1_in_rows, r + 1)
                    store_h1(r)

            turn(1, None)
            with sp.Fori(2, PAIRS - 1) as p:
                turn(p, p - 2)
            turn(PAIRS - 1, PAIRS - 3)
            for r in (PAIRS - 2, PAIRS - 1):
                sp.wait_ge(slots_ready, r + 1)
                sp.wait_ge(h1_in_rows, r + 1)
                store_h1(r)

            sp.wait_ge(rows_scattered, PAIRS * ROWS * 16)

            def expert_tiles(step, v):
                ep, i, u = step
                e = 2 * ep + v
                src = slots[e * CAPACITY:(e + 1) * CAPACITY, :].rearrange("(p n) r -> p n r", p=TILE)
                return src[:, bass.ds((i * SLOTS + u) * STEP_TILES, STEP_TILES), :]

            def load_xn(step):
                for v in range(2):
                    sp.dma_start(expert_xn[step[2]][:, :, v, :], expert_tiles(step, v)[:, :, 0:D])\
                        .then_inc(expert_xn_loaded[step[2]], 16)

            def load_rows(step):
                for v in range(2):
                    sp.dma_start(expert_rows[step[2]][:, v, :, :], expert_tiles(step, v)[:, :, D:ROW])\
                        .then_inc(rows_loaded[step[2]], 16)

            def load_ahead(step):
                if later(step, SLOTS):
                    sp.wait_ge(filled[TB], BASE[TB] + number(step) + 1)
                    load_xn(later(step, SLOTS))
                if later(step, 1):
                    sp.wait_ge(y_ready, number(step) - 1)
                    load_rows(later(step, 1))

            for u in range(SLOTS):
                load_xn((0, 0, u))
                load_rows((0, 0, u))
            for u in range(2):
                sp.wait_ge(filled[TB], BASE[TB] + u + 1)
                load_xn((0, 1, u))
            load_ahead((0, 0, 2))
            for ep in range(EXPERT_PAIRS):
                first = 1 if ep == 0 else 0
                with sp.Fori(first, TURNS - 1) as i:
                    for u in range(SLOTS):
                        load_ahead((ep, i, u))
                for u in range(SLOTS):
                    load_ahead((ep, TURNS - 1, u))

        @block.gpsimd
        def _(pool):
            for t in (embed_w, gcn_w, out_w, q1_w, k1_w, v_w, q2_w, k2_w):
                pool.memset(flat(t, t.shape[0], t.shape[1] * (t.shape[2] if len(t.shape) > 2 else 1)), 0.0)
            pool.memset(gate_w[:, :], 0.0).then_inc(zeroed, 1)
            pool.memset(blank, 0.0).then_inc(pool_steps, 1)
            pool.wait_ge(pool_steps, 1)
            pool.memset(blank.rearrange("p (n r) -> p n r", r=ROW)[:, :, ROW_TOK:ROW_TOK + 1].bitcast(I32), NOWHERE)\
                .then_inc(blank_ready, 1)
            pool.memset(h0[:, :, :, :].rearrange("p a b c -> p (a b c)"), 0.0).then_inc(zeroed, 1)
            pool.memset(w1[:, :, :, :].rearrange("p a b c -> p (a b c)"), 0.0)
            pool.memset(w2[:, :, :, :].rearrange("p a b c -> p (a b c)"), 0.0).then_inc(zeroed, 1)
            pool.memset(state[:, :, :].rearrange("p a b -> p (a b)"), 0.0).then_inc(zeroed, 1)
            pool.memset(rows[:, :, :].rearrange("p a b -> p (a b)"), 0.0).then_inc(zeroed, 1)
            pool.wait_ge(adj_ready, 1)
            pool.memset(phq_pad[:, :, :].rearrange("p a b -> p (a b)"), 0.0).then_inc(zeroed, 1)
            pool.memset(v_pad[:, :, :, :].rearrange("p a b c -> p (a b c)"), 0.0).then_inc(zeroed, 1)

            def pad_queries(q):
                for g, (c0, c1, n, t0) in enumerate(GROUPS):
                    w = (c1 - c0) * n
                    wait_apart(pool, phq_ready, 3 * q + g + 1, pool_waits)
                    for b in range(2):
                        half = slice(b * D, b * D + D)
                        ins = pool.tensor_scalar(phq_pad[half, b, t0:t0 + w], phq[half, t0:t0 + w], 1.0, 0.0,
                                                 ALU.mult, ALU.add)
                        ins.then_inc(phq_padded, 1)
                wait_apart(pool, phq_padded, 6 * q + 6, pool_waits)

            def scatter_rows(q):
                pool.wait_ge(slots_ready, q + 1)
                pool.wait_ge(h1_in_rows, q + 1)
                wait_apart(pool, norm_in_rows, q + 1, pool_waits)
                for r in range(ROWS):
                    n = tokens_in(r // 2)
                    pool.indirect_dma_start(
                        slots, bass.IndirectOffsetOnAxis(ap=slot_idx[0:n, r:r + 1], axis=0), rows[0:n, r, :], None,
                        bounds_check=EXPERTS * CAPACITY - 1, oob_is_err=False).then_inc(rows_scattered, 16)

            pool.wait_ge(zeroed, ZEROED)
            pool.wait_ge(blank_written, 16 * EXPERTS)
            pool.sem_inc(rows_free, 1)

            def route_rows(r):
                scatter_rows(r)
                pool.wait_ge(rows_scattered, (r + 1) * ROWS * 16)
                pool.wait_ge(h1_written, (r + 1) * 4 * 16)
                pool.sem_inc(rows_free, 1)

            pad_queries(0)
            with pool.Fori(1, PAIRS) as q:
                pad_queries(q)
                route_rows(q - 1)
            route_rows(PAIRS - 1)

            pool.wait_ge(h1_written, PAIRS * 4 * 16)
            with pool.Fori(0, EXPERT_PAIRS * TURNS) as m:
                for u in range(SLOTS):
                    wait_apart(pool, y_ready, m * SLOTS + u + 1, pool_waits)
                    for v in range(2):
                        for n in range(STEP_TILES):
                            pool.indirect_dma_start(
                                out, bass.IndirectOffsetOnAxis(
                                    ap=y_token[u][:, v * STEP_TILES + n:v * STEP_TILES + n + 1], axis=0),
                                y_out[u][:, v, n, :], None,
                                bounds_check=TOKENS - 1, oob_is_err=False).then_inc(y_scattered[u], 16)
            for u in range(SLOTS):
                pool.wait_ge(y_scattered[u], EXPERT_PAIRS * TURNS * 2 * STEP_TILES * 16)

        @block.scalar
        def _(act):
            def copy_tok_hw(p, l):
                for h, (s0, s1, _, _) in enumerate(HALVES):
                    tok_filled(act, p, f"hw{l}", h)
                    act.activation(hw[:, s0:s1, :],
                                   bank[A[h]][0:NODE_CHUNK, 0:(s1 - s0) * P].rearrange("p (s n) -> p s n", n=P),
                                   ACT.Copy).then_inc(drained[A[h]], 1)

            def att_columns(q, use, dst, func, col):
                for g, (c0, c1, n, t0) in enumerate(GROUPS):
                    w = (c1 - c0) * n
                    att_filled(act, q, use, g)
                    b = {} if col is None else {"bias": bias[:, col:col + 1]}
                    act.activation(dst[:, t0:t0 + w], bank[X[g]][:, 0:w], func, **b).then_inc(drained[X[g]], 1)

            def sines(q, src, dst, first, ready):
                for g, (c0, c1, n, t0) in enumerate(GROUPS):
                    w = (c1 - c0) * n
                    act.wait_ge(folded, 6 * q + first + g + 1)
                    act.activation(dst[:, t0:t0 + w], src[:, t0:t0 + w], ACT.Sin, bias=cst("sin_bias"),
                                   scale=cst("sin_scale")).then_inc(ready, 1)

            def step(p, q, r):
                if q is not None:
                    act.activation(junk[0][:, :], cst("sin_bias"), ACT.Silu)
                    att_columns(q, "xnT", xnT, ACT.Copy, None)
                    att_columns(q, "k1", h1k, ACT.Tanh, 5)
                    att_columns(q, "q1", h1q, ACT.Tanh, 4)
                if p is not None:
                    copy_tok_hw(p, 0)
                if q is not None:
                    att_columns(q, "k2", tk, ACT.Tanh, 7)
                    att_columns(q, "q2", tq, ACT.Tanh, 6)
                if r is not None:
                    att_columns(r, "xn2T", xnT, ACT.Copy, None)
                if p is not None:
                    copy_tok_hw(p, 1)
                if q is not None:
                    sines(q, tk, phk, 0, phk_ready)
                    sines(q, tq, phq, 3, phq_ready)
                if r is not None:
                    act.wait_ge(shifted_ready, r + 1)
                    act.activation(route[:, 1, :], route[:, 0, :], ACT.Exp).then_inc(exp_ready, 1)
                if q is not None:
                    for g, (c0, c1, n, _) in enumerate(GROUPS):
                        att_filled(act, q, "kT", g)
                        act.activation(phk_tok[0:n, c0:c1, :],
                                       bank[X[g]][0:n, 0:(c1 - c0) * P].rearrange("p (c n) -> p c n", n=P),
                                       ACT.Copy).then_inc(drained[X[g]], 1)
                if p is not None:
                    copy_tok_hw(p, 2)
                if r is not None:
                    act.wait_ge(rows_free, r + 1)
                    act.activation(rows[:, :, ROW_H:ROW_H + D], h1[:, :, :], ACT.Copy).then_inc(h1_in_rows, 1)
                if q is not None:
                    if r is not None:
                        act.wait_ge(h1_in_rows, r + 1)
                    act.activation(h1[:, :, :], h0[:, :, :, :].rearrange("p c b d -> p (c b) d"), ACT.Copy)\
                        .then_inc(h0_kept, 1)
                if r is not None:
                    act.wait_ge(xn2_ready, 3 * r + 3)
                    act.activation(rows[:, :, 0:D], xn[:, :, :, :].rearrange("p c b d -> p (c b) d"), ACT.Copy)\
                        .then_inc(norm_in_rows, 1)

            def write_blanks(experts):
                for e in experts:
                    part = slots[e * CAPACITY:(e + 1) * CAPACITY, :].rearrange("(p k m) r -> p k (m r)", p=TILE,
                                                                               m=BLANK_ROWS)
                    act.dma_start(part, blank.unsqueeze(1)
                                  .to_broadcast([TILE, TILES // BLANK_ROWS, BLANK_ROWS * ROW])).then_inc(blank_written, 16)

            act.wait_ge(consts_loaded, 16)
            act.wait_ge(blank_ready, 1)
            act.wait_ge(tok_w_loaded, TOK_LOADS * 16)
            write_blanks(range(0, EXPERTS // 2))
            step(0, None, None)
            write_blanks(range(EXPERTS // 2, EXPERTS))
            act.wait_ge(att_w_loaded, ATT_LOADS * 16)
            act.wait_ge(blank_written, 16 * EXPERTS)
            step(1, 0, None)
            with act.Fori(2, PAIRS) as it:
                step(it, it - 1, it - 2)
            step(None, PAIRS - 1, PAIRS - 2)
            step(None, None, PAIRS - 1)

            def copy_columns(step):
                act.wait_ge(filled[TB], BASE[TB] + number(step) + 1)
                act.activation(xT[step[2]], bank[TB][:, 0:STEP_COLS], ACT.Copy).then_inc(drained[TB], 1)

            def relu_hidden(step):
                for v, h in ((0, 0), (0, 1), (1, 0)):
                    b = HB[2 * v + h]
                    act.wait_ge(filled[b], BASE[b] + number(step) + 1)
                    act.activation(mid[step[2]][:, v, h, :], bank[b][:, 0:STEP_COLS], ACT.Relu,
                                   bias=b1_col[:, 2 * step[0] + v, h:h + 1]).then_inc(drained[b], 1)

            def expert_step(step):
                if later(step, 2):
                    copy_columns(later(step, 2))
                if later(step, 1):
                    relu_hidden(later(step, 1))

            act.wait_ge(expert_w_loaded, EXPERTS * 4 * 16)
            copy_columns((0, 0, 0))
            copy_columns((0, 0, 1))
            relu_hidden((0, 0, 0))
            for ep in range(EXPERT_PAIRS):
                with act.Fori(0, TURNS - 1) as i:
                    for u in range(SLOTS):
                        expert_step((ep, i, u))
                for u in range(SLOTS):
                    expert_step((ep, TURNS - 1, u))

        @block.tensor
        def _(pe):
            pe.wait_ge(far_ready, 1)
            pe.matmul(bank[7][0:1, 0:1], far_sum[:, :], ones[0:EDGE_P, 0:1], start=True, stop=True)\
                .then_inc(far_filled, 1)

            def count_edges(i, u, passes, windows, first):
                pe.wait_ge(hot_ready, (i + passes * EDGE_TURNS) * EDGE_UNROLL + u + 1)
                for s, (n0, n1) in enumerate(windows):
                    ins = pe.matmul(bank[s][0:NODE_CHUNK, 0:n1 - n0],
                                    hot_src[0:EDGE_P, u, s * NODE_CHUNK:(s + 1) * NODE_CHUNK],
                                    hot_dst[0:EDGE_P, u, n0:n1], start=first, stop=False)
                ins.then_inc(hot_used, 1)

            def count_all(passes, windows):
                for u in range(EDGE_UNROLL):
                    count_edges(0, u, passes, windows, u == 0)
                with pe.Fori(1, EDGE_TURNS) as i:
                    for u in range(EDGE_UNROLL):
                        count_edges(i, u, passes, windows, False)
                for s, (n0, n1) in enumerate(windows):
                    lo, hi = max(n0, s * NODE_CHUNK), min(n1, (s + 1) * NODE_CHUNK)
                    lo, hi = (lo, hi) if lo < hi else (n0, n0 + 1)
                    eye = (ident16[0:NODE_CHUNK, lo - s * NODE_CHUNK:hi - s * NODE_CHUNK]
                           if s * NODE_CHUNK <= lo < (s + 1) * NODE_CHUNK else zero16[0:NODE_CHUNK, 0:1])
                    ins = pe.matmul(bank[s][0:NODE_CHUNK, lo - n0:hi - n0], ident16[0:NODE_CHUNK, 0:NODE_CHUNK], eye,
                                    start=False, stop=True)
                ins.then_inc(counts_filled, 1)

            def normalize(near, embed_first):
                for t in range(NODE_CHUNKS):
                    if near:
                        pe.wait_ge(counts_drained, min(t + 2, NODE_CHUNKS))
                    sources = [s for s in range(NODE_CHUNKS) if abs(s - t) <= 1 or not near]
                    for s in sources:
                        ins = pe.matmul(bank[7][0:NODE_CHUNK, t:t + 1], adj[:, s, t * NODE_CHUNK:(t + 1) * NODE_CHUNK],
                                        ones[0:NODE_CHUNK, 0:1], start=(s == sources[0]), stop=(s == sources[-1]))
                ins.then_inc(degree_filled, 1)
                embed_first()
                pe.wait_ge(diag_ready, 1)
                for s in range(NODE_CHUNKS):
                    h = 0 if s < 4 else 1
                    at = (s - HALVES[h][0]) * NODE_CHUNK
                    ins = pe.matmul(bank[2 + h][0:P, at:at + NODE_CHUNK], ones[0:NODE_CHUNK, :], diag[:, s, :],
                                    start=True, stop=True)
                ins.then_inc(dinv_filled, 1)

            def embed(p):
                pe.wait_ge(image_loaded, (p + 1) * 12 * 16)
                for h in range(2):
                    tok_free(pe, p, "embed", h)
                    g0, g1 = ((0, 16), (16, 28))[h]
                    for m in range(4):
                        ins = pe.matmul(bank[A[h]][:, 0:(g1 - g0) * GRID], embed_w[:, m, :],
                                        image[:, g0:g1, 2 * m:SIDE:PATCH], start=(m == 0), stop=(m == 3))
                    ins.then_inc(filled[A[h]], 1)

            def node_products(p, use, w):
                for h, (s0, s1, _, _) in enumerate(HALVES):
                    tok_free(pe, p, use, h)
                    for s in range(s0, s1):
                        ins = pe.matmul(bank[A[h]][0:NODE_CHUNK, (s - s0) * P:(s - s0 + 1) * P],
                                        hT[:, s * NODE_CHUNK:(s + 1) * NODE_CHUNK], w, start=True, stop=True)
                    ins.then_inc(filled[A[h]], 1)

            def aggregate(p, l, h, banded):
                if h == 0:
                    for k in range(2):
                        tok_free(pe, p, f"agg{l}", k)
                    if isinstance(p, int) and p == 0:
                        pe.wait_ge(adj_ready, 1)
                d0, d1, n0, w = HALVES[h]
                if banded:
                    for d in range(d0, d1):
                        near = range(max(d - 1, 0), min(d + 2, NODE_CHUNKS))
                        for s in near:
                            ins = pe.matmul(bank[A[h]][:, (d - d0) * NODE_CHUNK:(d - d0 + 1) * NODE_CHUNK], hw[:, s, :],
                                            adj[:, s, d * NODE_CHUNK:(d + 1) * NODE_CHUNK],
                                            start=(s == near[0]), stop=(s == near[-1]))
                else:
                    for s in range(NODE_CHUNKS):
                        ins = pe.matmul(bank[A[h]][:, 0:w], hw[:, s, :], adj[:, s, n0:n0 + w],
                                        start=(s == 0), stop=(s == NODE_CHUNKS - 1))
                ins.then_inc(filled[A[h]], 1)

            def turn_tokens(q, use, src, ready):
                for g, (c0, c1, n, _) in enumerate(GROUPS):
                    pe.wait_ge(ready, 3 * q + g + 1)
                    att_free(pe, q, use, g)
                    for c in range(c0, c1):
                        ins = pe.transpose(bank[X[g]][:, (c - c0) * n:(c - c0 + 1) * n], src(c, n),
                                           cst("ident")[0:n, 0:n])
                    ins.then_inc(filled[X[g]], 1)

            def project(q, use, w, src):
                for g, (c0, c1, n, t0) in enumerate(GROUPS):
                    cols = (c1 - c0) * n
                    att_free(pe, q, use, g)
                    ins = pe.matmul(bank[X[g]][:, 0:cols], w[:, :], src[:, t0:t0 + cols], start=True, stop=True)
                    ins.then_inc(filled[X[g]], 1)

            def values(q):
                for g, (c0, c1, n, _) in enumerate(GROUPS):
                    att_free(pe, q, "v", g)
                    for c in range(c0, c1):
                        t = first_token(c)
                        ins = pe.matmul(bank[X[g]][0:n, (c - c0) * P:(c - c0 + 1) * P], xnT[:, t:t + n], v_w[:, :],
                                        start=True, stop=True)
                    ins.then_inc(filled[X[g]], 1)

            def key_rows(q):
                for g, (c0, c1, n, _) in enumerate(GROUPS):
                    att_free(pe, q, "kT", g)
                    pe.wait_ge(phk_ready, 3 * q + g + 1)
                    for c in range(c0, c1):
                        t = first_token(c)
                        ins = pe.transpose(bank[X[g]][0:n, (c - c0) * P:(c - c0 + 1) * P], phk[:, t:t + n],
                                           cst("ident"))
                    ins.then_inc(filled[X[g]], 1)

            def key_values(q):
                for g, (c0, c1, n, _) in enumerate(GROUPS):
                    att_free(pe, q, "kv", g)
                    for c in range(c0, c1):
                        ins = pe.matmul(bank[X[g]][:, (c - c0) * P:(c - c0 + 1) * P], phk_tok[0:n, c, :],
                                        v_pad[0:n, c, 0:4:3, :], start=True, stop=True)
                    ins.then_inc(filled[X[g]], 1)

            def scores(q, f):
                score_free(pe, q, f)
                g = 0 if f < 2 else 1 if f < 4 else 2
                pe.wait_ge(phq_padded, 6 * q + 2 * g + 2)
                for j, c in enumerate(SCORE_FILLS[f]):
                    t, n = first_token(c), tokens_in(c)
                    ins = pe.matmul(score_view(f, n)[:, 2 * j:2 * j + 2, :], phk[:, t:t + n],
                                    phq_pad[:, :, t:t + n], start=True, stop=True)
                ins.then_inc(filled[S[f % 2]], 1)

            def retrieve(q, f):
                score_drained(pe, q, f)
                for j, c in enumerate(SCORE_FILLS[f]):
                    t, n = first_token(c), tokens_in(c)
                    g = [i for i, G in enumerate(GROUPS) if G[0] <= c < G[1]][0]
                    c0, c1 = GROUPS[g][0:2]
                    if c == c0:
                        att_free(pe, q, "out", g)
                    o = bank[X[g]][0:n, (c - c0) * P:(c - c0 + 1) * P]
                    if c:
                        pe.matmul(o, phq[:, t:t + n], state[:, c, :], start=True, stop=False)
                    for b in range(2):
                        ins = pe.matmul(o, masked[0:n, f % 3, 2 * j + b, 0:n], v_pad[0:n, c, 2 * b:2 * b + 2, :],
                                        start=(c == 0 and b == 0), stop=(b == 1))
                    if c == c1 - 1:
                        ins.then_inc(filled[X[g]], 1)

            def gates(q):
                route_free(pe, q, 0)
                for c in range(CHUNKS):
                    if c in (0, 4, 7):
                        att_drained(pe, q, "xn2T", (0, 4, 7).index(c))
                    t, n = first_token(c), tokens_in(c)
                    ins = pe.matmul(bank[R][0:n, 16 * c:16 * c + 16], xnT[:, t:t + n], gate_w[:, :],
                                    start=True, stop=True)
                ins.then_inc(filled[R], 1)

            def counts(q):
                route_free(pe, q, 1)
                pe.wait_ge(onehot_ready, q + 1)
                nodes, all_cols = NODE_CHUNKS * 2 * EXPERTS, ROWS * EXPERTS
                for k, lhs in enumerate((causal16, ones16)):
                    for n, lo, hi in ((NODE_CHUNK, 0, nodes), (TEXT_CHUNK, nodes, all_cols)):
                        ins = pe.matmul(bank[R][:, k * all_cols + lo:k * all_cols + hi], lhs[0:n, :],
                                        onehot16[0:n, lo:hi], start=True, stop=True)
                ins.then_inc(filled[R], 1)

            def step(p, q, r, banded):
                if p is not None and not (isinstance(p, int) and p == 0):
                    embed(p)
                if q is not None:
                    turn_tokens(q, "xnT", lambda c, n: xn[0:n, c, :, :].rearrange("p b d -> p (b d)"),
                                xn_ready)
                    project(q, "k1", k1_w, xnT)
                    project(q, "q1", q1_w, xnT)
                if p is not None:
                    node_products(p, "hw0", gcn_w[:, 0, :])
                if q is not None:
                    values(q)
                    project(q, "k2", k2_w, h1k)
                    project(q, "q2", q2_w, h1q)
                if p is not None:
                    aggregate(p, 0, 0, banded)
                    aggregate(p, 0, 1, banded)
                if r is not None:
                    turn_tokens(r, "xn2T", lambda c, n: xn2[0:n, c, :], xn2_ready)
                if p is not None:
                    node_products(p, "hw1", gcn_w[:, 1, :])
                if r is not None:
                    gates(r)
                if q is not None:
                    key_rows(q)
                if p is not None:
                    aggregate(p, 1, 0, banded)
                    aggregate(p, 1, 1, banded)
                if q is not None:
                    key_values(q)
                if p is not None:
                    node_products(p, "hw2", gcn_w[:, 2, :])
                if q is not None:
                    scores(q, 0)
                    scores(q, 1)
                if p is not None:
                    aggregate(p, 2, 0, banded)
                if r is not None:
                    counts(r)
                if p is not None:
                    aggregate(p, 2, 1, banded)
                if q is not None:
                    retrieve(q, 0)
                    scores(q, 2)
                if p is not None:
                    node_products(p, "out", out_w[:, :])
                if q is not None:
                    for f in range(1, 6):
                        retrieve(q, f)
                        if f + 2 < 6:
                            scores(q, f + 2)

            def pairs(banded):
                pe.wait_ge(tok_w_loaded, TOK_LOADS * 16)
                step(0, None, None, banded)
                pe.wait_ge(att_w_loaded, ATT_LOADS * 16)
                pe.wait_ge(zeroed, ZEROED)
                step(1, 0, None, banded)
                with pe.Fori(2, PAIRS) as it:
                    step(it, it - 1, it - 2, banded)

            def first_embedding():
                pe.wait_ge(embed_w_loaded, EMBED_LOADS * 16)
                embed(0)

            pe.wait_ge(far_known, 1)
            with pe.If(pe.value_load(far_edges[0:1, 0:1]) == 0):
                count_all(0, NEAR_WINDOWS)
                normalize(True, first_embedding)
                pairs(True)
            with pe.Else():
                for half in range(2):
                    if half:
                        pe.wait_ge(counts_drained, NODE_CHUNKS)
                    count_all(half, [(half * HALF_NODES, (half + 1) * HALF_NODES)] * NODE_CHUNKS)
                pe.wait_ge(counts_drained, 2 * NODE_CHUNKS)
                normalize(False, first_embedding)
                pairs(False)
            step(None, PAIRS - 1, PAIRS - 2, False)
            step(None, None, PAIRS - 1, False)

            pe.wait_ge(expert_w_loaded, EXPERTS * 4 * 16)

            def turn_rows(step):
                n, u = number(step), step[2]
                pe.wait_ge(expert_xn_loaded[u], (step[1] + step[0] * TURNS + 1) * 2 * 16)
                pe.wait_ge(drained[TB], BASE[TB] + n + 1)
                for k in range(STEP_TILES):
                    ins = pe.transpose(bank[TB][:, k * TILE:(k + 1) * TILE],
                                       expert_xn[u][:, k, :, :].rearrange("p v d -> p (v d)"),
                                       cst("ident")[0:TILE, 0:TILE])
                ins.then_inc(filled[TB], 1)

            def up(step):
                n, u = number(step), step[2]
                pe.wait_ge(drained[TB], BASE[TB] + n + 2)
                for v in range(2):
                    for h in range(2):
                        b = HB[2 * v + h]
                        pe.wait_ge(drained[b], BASE[b] + n + 1)
                        pe.matmul(bank[b][:, 0:STEP_COLS], w1[:, step[0], v, h * P:(h + 1) * P], xT[u],
                                  start=True, stop=True).then_inc(filled[b], 1)

            def down(step):
                n, u = number(step), step[2]
                for v in range(2):
                    pe.wait_ge(drained[YB[v]], BASE[YB[v]] + n + 1)
                    for h in range(2):
                        b = HB[2 * v + h]
                        pe.wait_ge(drained[b], BASE[b] + n + 2)
                    for k in range(STEP_TILES):
                        for h in range(2):
                            ins = pe.matmul(bank[YB[v]][0:TILE, k * P:(k + 1) * P],
                                            mid[u][:, v, h, k * TILE:(k + 1) * TILE], w2[:, 2 * step[0] + v, h, :],
                                            start=(h == 0), stop=(h == 1))
                    ins.then_inc(filled[YB[v]], 1)

            def expert_step(step):
                if later(step, 2):
                    turn_rows(later(step, 2))
                if later(step, 1):
                    up(later(step, 1))
                down(step)

            turn_rows((0, 0, 0))
            turn_rows((0, 0, 1))
            up((0, 0, 0))
            for ep in range(EXPERT_PAIRS):
                with pe.Fori(0, TURNS - 1) as i:
                    for u in range(SLOTS):
                        expert_step((ep, i, u))
                for u in range(SLOTS):
                    expert_step((ep, TURNS - 1, u))

        @block.vector
        def _(dve):
            steps = Steps(dve, dve_steps)
            done, settle = steps.done, steps.settle

            def rsqrt(y, v, vh, t):
                done(dve.tensor_scalar(vh, v, -0.5, None, ALU.mult))
                done(dve.tensor_scalar(y.bitcast(I32), v.bitcast(I32), -0.5, RSQRT_SEED, ALU.mult, ALU.add))
                settle()
                for _ in range(3):
                    done(dve.tensor_tensor(t, y, y, ALU.mult))
                    settle()
                    done(dve.tensor_tensor(t, t, vh, ALU.mult))
                    settle()
                    done(dve.scalar_tensor_tensor(y, t, 1.5, y, ALU.add, ALU.mult))
                    settle()

            steps = Steps(dve, setup_steps)
            done, settle = steps.done, steps.settle
            dve.wait_ge(edges_loaded, 16)
            done(dve.tensor_copy(edges_f[:, :, :], edges_i[:, :, :]))
            done(dve.memset(ones[:, :], 1.0))
            settle()
            done(dve.tensor_scalar(edge_block[:, :, :], edges_f[:, :, :], float(NODE_CHUNK), None, ALU.is_ge))
            for s in range(2, NODE_CHUNKS):
                settle()
                done(dve.scalar_tensor_tensor(edge_block[:, :, :], edges_f[:, :, :], float(s * NODE_CHUNK),
                                              edge_block[:, :, :], ALU.is_ge, ALU.add))
            settle()
            apart = edge_block[:, 0, :]
            done(dve.tensor_tensor(apart, apart, edge_block[:, 1, :], ALU.subtract))
            settle()
            done(dve.tensor_tensor(apart, apart, apart, ALU.mult))
            settle()
            done(dve.tensor_scalar(apart, apart, 1.0, None, ALU.is_gt))
            settle()
            dve.tensor_reduce(far_sum[:, :], apart, AX.X, ALU.add).then_inc(far_ready, 1)
            dve.wait_ge(consts_loaded, 16)
            done(dve.tensor_copy(nodes16, cst("nodes")))
            done(dve.tensor_copy(ident16[:, :], cst("ident")))
            done(dve.memset(zero16[:, :], 0.0))
            dve.wait_ge(far_filled, 1)
            dve.tensor_copy(far_edges[:, :], bank[7][0:1, 0:1]).then_inc(far_known, 1)
            settle()

            def one_hot(i, u):
                dve.tensor_scalar(hot_src[0:EDGE_P, u, :], nodes16[0:EDGE_P, :],
                                  edges_f[:, 0, bass.ds(i * EDGE_UNROLL + u, 1)], None, ALU.is_equal)
                dve.tensor_scalar(hot_dst[0:EDGE_P, u, :], nodes16[0:EDGE_P, :],
                                  edges_f[:, 1, bass.ds(i * EDGE_UNROLL + u, 1)], None, ALU.is_equal)\
                    .then_inc(hot_ready, 1)

            def more_one_hots(passes):
                with dve.Fori(1, EDGE_TURNS) as i:
                    for u in range(EDGE_UNROLL):
                        dve.wait_ge(hot_used, (i - 1 + passes * EDGE_TURNS) * EDGE_UNROLL + u + 1)
                        one_hot(i, u)

            def take_counts(passes, windows):
                dve.wait_ge(counts_filled, passes + 1)
                for s, (n0, n1) in enumerate(windows):
                    dve.tensor_copy(adj[:, s, n0:n1], bank[s][0:NODE_CHUNK, 0:n1 - n0]).then_inc(counts_drained, 1)

            def store_embedding(p):
                for h, (_, _, n0, w) in enumerate(HALVES):
                    tok_filled(dve, p, "embed", h)
                    dve.tensor_tensor(hT[:, n0:n0 + w], bank[A[h]][:, 0:w], pos_b[:, n0:n0 + w], ALU.add)\
                        .then_inc(drained[A[h]], 1)

            def scale_counts(windows):
                deg, dinv, vh, t = (small[0:NODE_CHUNK, k, 0:NODE_CHUNKS] for k in range(4))
                dve.wait_ge(tok_w_loaded, TOK_LOADS * 16)
                done(dve.tensor_scalar(pos_b[:, :], cst("position"), bias[:, 0:1], None, ALU.add))
                dve.wait_ge(degree_filled, 1)
                done(dve.tensor_copy(deg, bank[7][0:NODE_CHUNK, 0:NODE_CHUNKS]))
                settle()
                rsqrt(dinv, deg, vh, t)
                for s in range(NODE_CHUNKS):
                    ins = dve.tensor_scalar(diag[:, s, :], cst("ident", NODE_CHUNK)[:, 0:NODE_CHUNK], dinv[:, s:s + 1],
                                            None, ALU.mult)
                ins.then_inc(diag_ready, 1)
                store_embedding(0)
                dve.wait_ge(dinv_filled, 1)
                for s, (n0, n1) in enumerate(windows):
                    for h, (_, _, h0_, w) in enumerate(HALVES):
                        lo, hi = max(n0, h0_), min(n1, h0_ + w)
                        if lo < hi:
                            ins = dve.scalar_tensor_tensor(adj[:, s, lo:hi], adj[:, s, lo:hi], dinv[:, s:s + 1],
                                                           bank[2 + h][0:NODE_CHUNK, lo - h0_:hi - h0_],
                                                           ALU.mult, ALU.mult)
                ins.then_inc(adj_ready, 1)

            for u in range(EDGE_UNROLL):
                one_hot(0, u)
            dve.wait_ge(far_known, 1)
            with dve.If(dve.value_load(far_edges[0:1, 0:1]) == 0):
                more_one_hots(0)
                take_counts(0, NEAR_WINDOWS)
                dve.wait_ge(counts_drained, NODE_CHUNKS)
                for h in range(2):
                    dve.sem_inc(drained[A[h]], 1)
                scale_counts(NEAR_WINDOWS)
            with dve.Else():
                for half in range(2):
                    if half:
                        for u in range(EDGE_UNROLL):
                            dve.wait_ge(hot_used, (EDGE_TURNS - 1) * EDGE_UNROLL + u + 1)
                            one_hot(0, u)
                    more_one_hots(half)
                    take_counts(half, [(half * HALF_NODES, (half + 1) * HALF_NODES)] * NODE_CHUNKS)
                dve.wait_ge(counts_drained, 2 * NODE_CHUNKS)
                for h in range(2):
                    dve.sem_inc(drained[A[h]], 1)
                scale_counts([(0, NODES)] * NODE_CHUNKS)

            steps = Steps(dve, dve_steps)
            done, settle = steps.done, steps.settle
            done(dve.tensor_copy(causal16[:, :], cst("causal")))
            done(dve.memset(ones16[:, :], 1.0))
            done(dve.memset(base[:, :], 0.0))
            done(dve.memset(route[:, :, :].rearrange("p a b -> p (a b)"), 0.0))
            dve.wait_ge(adj_ready, 1)
            for b in range(8):
                if b not in A:
                    dve.sem_inc(drained[b], 1)
            settle()
            dve.wait_ge(zeroed, 2)

            def row_stats(src, r0, r1):
                for r in range(r0, r1):
                    done(dve.bn_stats(stats[:, r, :], src[:, r, :]))

            def layer_norm(src, dst, ready, between=None):
                settle()
                me, mo, se, so = (stats[:, :, k] for k in (1, 4, 2, 5))
                mean, dm, var, t, y, vh = (small[:, k, :] for k in range(6))
                done(dve.tensor_tensor(mean, me, mo, ALU.add))
                done(dve.tensor_tensor(dm, me, mo, ALU.subtract))
                done(dve.tensor_tensor(var, se, so, ALU.add))
                settle()
                done(dve.tensor_scalar(mean, mean, 0.5, None, ALU.mult))
                done(dve.tensor_tensor(dm, dm, dm, ALU.mult))
                done(dve.tensor_scalar(var, var, 1.0 / D, LN_EPS, ALU.mult, ALU.add))
                settle()
                wide = mean.unsqueeze(2).to_broadcast([P, ROWS, D])
                done(dve.tensor_tensor(dst, src, wide, ALU.subtract))
                done(dve.scalar_tensor_tensor(var, dm, 0.25, var, ALU.mult, ALU.add))
                settle()
                if between:
                    between()
                rsqrt(y, var, vh, t)
                for c0, c1, _, _ in GROUPS:
                    part = slice(2 * c0, 2 * c1)
                    dve.tensor_tensor(dst[:, part, :], dst[:, part, :],
                                      y[:, part].unsqueeze(2).to_broadcast([P, 2 * (c1 - c0), D]), ALU.mult)\
                        .then_inc(ready, 1)

            h0_rows = h0[:, :, :, :].rearrange("p c b d -> p (c b) d")
            xn_rows = xn[:, :, :, :].rearrange("p c b d -> p (c b) d")

            def relu_nodes(p, l):
                for h, (_, _, n0, w) in enumerate(HALVES):
                    tok_filled(dve, p, f"agg{l}", h)
                    dve.tensor_scalar(hT[:, n0:n0 + w], bank[A[h]][:, 0:w], bias[:, l + 1:l + 2], 0.0,
                                      ALU.add, ALU.max).then_inc(drained[A[h]], 1)

            def store_nodes(p):
                if not (isinstance(p, int) and p == 0):
                    dve.wait_ge(h0_kept, p)
                for h, (s0, s1, _, _) in enumerate(HALVES):
                    tok_filled(dve, p, "out", h)
                    dve.tensor_tensor(h0[0:NODE_CHUNK, s0:s1, :, :],
                                      bank[A[h]][0:NODE_CHUNK, 0:(s1 - s0) * P]
                                      .rearrange("p (s b d) -> p s b d", b=2, d=D),
                                      out_b[0:NODE_CHUNK].unsqueeze(1).to_broadcast([NODE_CHUNK, s1 - s0, 2, D]),
                                      ALU.add).then_inc(drained[A[h]], 1)

            def text_stats(p):
                dve.wait_ge(text_loaded, (p + 1) * 2 * 16)
                row_stats(h0_rows, 2 * NODE_CHUNKS, ROWS)

            def node_stats(p, h):
                dve.wait_ge(drained[A[h]], (p + 1) * len(TOK_USES) + 1)
                row_stats(h0_rows, 2 * HALVES[h][0], 2 * HALVES[h][1])

            def store_values(q):
                for g, (c0, c1, n, _) in enumerate(GROUPS):
                    att_filled(dve, q, "v", g)
                    dve.tensor_tensor(v_pad[0:n, c0:c1, 0:4:3, :],
                                      bank[X[g]][0:n, 0:(c1 - c0) * P].rearrange("p (c b d) -> p c b d", b=2, d=D),
                                      v_b[0:n].unsqueeze(1).to_broadcast([n, c1 - c0, 2, D]),
                                      ALU.add).then_inc(drained[X[g]], 1)

            def fold(q, use, t):
                for g, (c0, c1, n, t0) in enumerate(GROUPS):
                    w = (c1 - c0) * n
                    att_drained(dve, q, use, g)
                    dve.scalar_tensor_tensor(t[:, t0:t0 + w], t[:, t0:t0 + w], cst("fold"), t[:, t0:t0 + w],
                                             ALU.mult, ALU.max).then_inc(folded, 1)

            def add_states(q):
                for g, (c0, c1, _, _) in enumerate(GROUPS):
                    att_filled(dve, q, "kv", g)
                    for c in range(c0, c1):
                        at = (c - c0) * P
                        if c < CHUNKS - 1:
                            for b in range(2):
                                half = slice(b * D, b * D + D)
                                new, part = state[half, c + 1, half], bank[X[g]][half, at + b * D:at + b * D + D]
                                if c == 0:
                                    done(dve.tensor_copy(new, part))
                                else:
                                    done(dve.tensor_tensor(new, part, state[half, c, half], ALU.add))
                            settle()
                    dve.tensor_copy(junk[1][:, :], bank[X[g]][:, 0:1]).then_inc(drained[X[g]], 1)

            def mask_scores(q, f):
                score_filled(dve, q, f)
                n, k = tokens_in(SCORE_FILLS[f][0]), 2 * len(SCORE_FILLS[f])
                dve.tensor_tensor(masked[0:n, f % 3, 0:k, 0:n], score_view(f, n)[:, 0:k, :],
                                  cst("causal", n)[:, 0:n].unsqueeze(1).to_broadcast([n, k, n]), ALU.mult)\
                    .then_inc(drained[S[f % 2]], 1)

            def add_retrieved(q, g):
                c0, c1, n, _ = GROUPS[g]
                att_filled(dve, q, "out", g)
                dve.wait_ge(h0_kept, q + 1)
                for c in range(c0, c1):
                    ins = dve.scalar_tensor_tensor(
                        h1[0:n, 2 * c:2 * c + 2, :],
                        bank[X[g]][0:n, (c - c0) * P:(c - c0 + 1) * P].rearrange("p (b d) -> p b d", b=2),
                        cst("rnorm", n)[:, c:c + 1], h1[0:n, 2 * c:2 * c + 2, :], ALU.mult, ALU.add)
                ins.then_inc(drained[X[g]], 1)

            def h1_stats(r):
                for g in range(3):
                    att_drained(dve, r, "out", g)
                row_stats(h1, 0, ROWS)

            def by_expert(k):
                return route[:, k, :].rearrange("p (r e) -> p r e", e=EXPERTS)

            def wide(x):
                return x.unsqueeze(2).to_broadcast([P, ROWS, EXPERTS])

            def wide_e(x):
                return x.unsqueeze(1).to_broadcast([P, ROWS, EXPERTS])

            def shift_logits(q):
                route_filled(dve, q, 0)
                for n, c0, c1 in ((NODE_CHUNK, 0, NODE_CHUNKS), (TEXT_CHUNK, NODE_CHUNKS, CHUNKS)):
                    ins = dve.tensor_tensor(route[0:n, 2, 16 * c0:16 * c1].rearrange("p (c k) -> p c k", k=16),
                                            bank[R][0:n, 16 * c0:16 * c1].rearrange("p (c k) -> p c k", k=16),
                                            gate_b[0:n].rearrange("p b e -> p (b e)").unsqueeze(1)
                                            .to_broadcast([n, c1 - c0, 16]), ALU.add)
                    if c0:
                        ins.then_inc(drained[R], 1)
                    else:
                        done(ins)
                route_drained(dve, q, 0)
                settle()
                done(dve.tensor_reduce(small[:, 6, :], by_expert(2), AX.X, ALU.max))
                settle()
                dve.tensor_tensor(by_expert(0), by_expert(2), wide(small[:, 6, :]), ALU.subtract).then_inc(shifted_ready, 1)

            def choose(q):
                dve.wait_ge(exp_ready, q + 1)
                total, inv, prb, idx = (small[:, k, :] for k in (7, 8, 9, 10))
                done(dve.tensor_reduce(total, by_expert(1), AX.X, ALU.add))
                settle()
                done(dve.reciprocal(inv, total))
                settle()
                done(dve.tensor_tensor(by_expert(2), by_expert(1), wide(inv), ALU.mult))
                settle()
                done(dve.tensor_reduce(prb, by_expert(2), AX.X, ALU.max))
                settle()
                done(dve.tensor_tensor(by_expert(3), by_expert(2), wide(prb), ALU.is_ge))
                dve.wait_ge(rows_free, q + 1)
                done(dve.tensor_copy(rows[:, :, ROW_PRB], prb))
                settle()
                done(dve.tensor_tensor(by_expert(3), by_expert(3), wide_e(cst("expert_less_8")), ALU.mult))
                settle()
                done(dve.tensor_reduce(idx, by_expert(3), AX.X, ALU.min))
                settle()
                done(dve.tensor_tensor(by_expert(4), wide_e(cst("expert_less_8")), wide(idx), ALU.is_equal))
                settle()
                dve.tensor_copy(onehot16[:, :], route[:, 4, :]).then_inc(onehot_ready, 1)

            def place(q):
                route_filled(dve, q, 1)
                n = ROWS * EXPERTS
                order = "p (c b e) -> p e b c"
                done(dve.tensor_copy(route[:, 5, :].rearrange("p (e b c) -> p e b c", e=EXPERTS, b=2),
                                     bank[R][:, n:2 * n].rearrange(order, b=2, e=EXPERTS)))
                settle()
                done(dve.tensor_tensor_scan(route[:, 6, :], cst("carry"), route[:, 5, :], 0.0, ALU.mult, ALU.add))
                settle()
                done(dve.tensor_tensor(route[:, 5, :], route[:, 6, :], route[:, 5, :], ALU.subtract))
                settle()
                b3 = route[:, 5, :].rearrange("p (e r) -> p e r", e=EXPERTS)
                done(dve.tensor_tensor(b3, b3, base[:, :].unsqueeze(2).to_broadcast([P, EXPERTS, ROWS]), ALU.add))
                settle()
                done(dve.tensor_tensor(base[:, :], base[:, :],
                                       route[:, 6, :].rearrange("p (e r) -> p e r", e=EXPERTS)[:, :, ROWS - 1], ALU.add))
                dve.tensor_tensor(route[:, 7, :].rearrange("p (c b e) -> p c b e", b=2, e=EXPERTS)[:, :, 0, :],
                                  bank[R][:, 0:n].rearrange("p (c b e) -> p c b e", b=2, e=EXPERTS)[:, :, 0, :],
                                  route[:, 5, :].rearrange("p (e b c) -> p c b e", e=EXPERTS, b=2)[:, :, 0, :], ALU.add)
                dve.tensor_tensor(route[:, 7, :].rearrange("p (c b e) -> p c b e", b=2, e=EXPERTS)[:, :, 1, :],
                                  bank[R][:, 0:n].rearrange("p (c b e) -> p c b e", b=2, e=EXPERTS)[:, :, 1, :],
                                  route[:, 5, :].rearrange("p (e b c) -> p c b e", e=EXPERTS, b=2)[:, :, 1, :], ALU.add)\
                    .then_inc(drained[R], 1)
                route_drained(dve, q, 1)
                done(dve.tensor_scalar(route[:, 6, :], route[:, 7, :], float(CAPACITY), float(NOWHERE), ALU.is_gt, ALU.mult))
                done(dve.tensor_tensor(by_expert(7), by_expert(7), wide_e(cst("slot_base")), ALU.add))
                settle()
                done(dve.tensor_tensor(route[:, 7, :], route[:, 7, :], route[:, 6, :], ALU.add))
                settle()
                done(dve.tensor_tensor(route[:, 7, :], route[:, 7, :], route[:, 4, :], ALU.mult))
                settle()
                done(dve.tensor_reduce(small[:, 11, :], by_expert(7), AX.X, ALU.add))
                done(dve.tensor_copy(rows[:, :, ROW_TOK].bitcast(I32), cst("token")))
                settle()
                done(dve.tensor_scalar(cst("token"), cst("token"), float(2 * L), None, ALU.add))
                dve.tensor_copy(slot_idx[:, :], small[:, 11, :]).then_inc(slots_ready, 1)
                settle()

            def step(p, q, r):
                if p is not None and not (isinstance(p, int) and p == 0):
                    store_embedding(p)
                if r is not None:
                    h1_stats(r)
                if q is not None:
                    store_values(q)
                if r is not None:
                    if q is not None:
                        att_filled(dve, q, "xnT", 2)
                    else:
                        dve.wait_ge(norm_in_rows, r)
                    layer_norm(h1[:, :, :], xn_rows, xn2_ready, q is not None and (lambda: fold(q, "k2", tk)))
                elif q is not None:
                    fold(q, "k2", tk)
                if p is not None:
                    relu_nodes(p, 0)
                if q is not None:
                    fold(q, "q2", tq)
                if r is not None:
                    shift_logits(r)
                if p is not None:
                    relu_nodes(p, 1)
                if r is not None:
                    choose(r)
                if q is not None:
                    add_states(q)
                if r is not None and p is None:
                    place(r)
                if q is not None:
                    mask_scores(q, 0)
                    mask_scores(q, 1)
                if p is not None:
                    relu_nodes(p, 2)
                if q is not None:
                    mask_scores(q, 2)
                if p is not None:
                    store_nodes(p)
                    text_stats(p)
                if q is not None:
                    mask_scores(q, 3)
                    add_retrieved(q, 0)
                    mask_scores(q, 4)
                if p is not None:
                    node_stats(p, 0)
                if q is not None:
                    mask_scores(q, 5)
                    add_retrieved(q, 1)
                if p is not None:
                    node_stats(p, 1)
                if q is not None:
                    add_retrieved(q, 2)
                if p is not None:
                    if r is not None:
                        dve.wait_ge(norm_in_rows, r + 1)
                    layer_norm(h0_rows, xn_rows, xn_ready)
                if r is not None and p is not None:
                    place(r)

            step(0, None, None)
            dve.wait_ge(zeroed, ZEROED)
            step(1, 0, None)
            total = steps.n
            with dve.Fori(2, PAIRS) as it:
                steps.begin((it - 2) * LOOP_STEPS + total)
                step(it, it - 1, it - 2)
                assert steps.n == LOOP_STEPS, steps.n
            steps.begin(total + (PAIRS - 2) * LOOP_STEPS)
            step(None, PAIRS - 1, PAIRS - 2)
            step(None, None, PAIRS - 1)
            total = steps.base + steps.n

            def relu_hidden(step):
                b = HB[3]
                dve.wait_ge(filled[b], BASE[b] + number(step) + 1)
                dve.tensor_scalar(mid[step[2]][:, 1, 1, :], bank[b][:, 0:STEP_COLS],
                                  b1_col[:, 2 * step[0] + 1, 1:2], 0.0, ALU.add, ALU.max).then_inc(drained[b], 1)

            def expert_step(step):
                if later(step, 1):
                    relu_hidden(later(step, 1))
                ep, i, u = step
                m = i + ep * TURNS
                n = number(step)
                y, low, high, fin = y_work
                for v in range(2):
                    e = 2 * ep + v
                    dve.wait_ge(filled[YB[v]], BASE[YB[v]] + n + 1)
                    dve.tensor_tensor(y[:, v], bank[YB[v]][0:TILE, 0:STEP_TILES * P]
                                      .rearrange("p (k n) -> p k n", n=P)[:, :, 0:D],
                                      b2_row[0:TILE, e, :].unsqueeze(1).to_broadcast([TILE, STEP_TILES, D]),
                                      ALU.add).then_inc(drained[YB[v]], 1)
                for v in range(2):
                    dve.wait_ge(drained[YB[v]], BASE[YB[v]] + n + 2)
                er = expert_rows[u][:, :, :, :].rearrange("p v k r -> p (v k) r")
                yf, lf, hf, ff = (t.rearrange("p v k d -> p (v k) d") for t in (y, low, high, fin))
                dve.wait_ge(rows_loaded[u], (m + 1) * 2 * 16)
                done(dve.tensor_tensor(yf, yf, er[:, :, ROW_PRB - D:ROW_PRB + 1 - D].to_broadcast([TILE, 6, D]), ALU.mult))
                settle()
                done(dve.tensor_scalar(lf, yf, 0.0, -1e4, ALU.min, ALU.max))
                done(dve.tensor_scalar(hf, yf, 0.0, 1e4, ALU.max, ALU.min))
                done(dve.tensor_scalar(ff.bitcast(I32), yf, 0.0, 0.0, ALU.mult, ALU.is_equal))
                settle()
                done(dve.tensor_tensor(lf, lf, hf, ALU.add))
                wait_apart(dve, dve_steps, steps.base + steps.n, dve_waits)
                done(dve.copy_predicated(lf, ff.bitcast(I32), yf))
                settle()
                if not (isinstance(m, int) and m == 0):
                    dve.wait_ge(y_scattered[u], m * 2 * STEP_TILES * 16)
                done(dve.tensor_copy(y_token[u][:, :], er[:, :, ROW_TOK - D].bitcast(I32)))
                settle()
                dve.tensor_tensor(y_out[u].rearrange("p v k d -> p (v k) d"), lf, er[:, :, 0:D], ALU.add)\
                    .then_inc(y_ready, 1)

            dve.wait_ge(expert_w_loaded, EXPERTS * 4 * 16)
            relu_hidden((0, 0, 0))
            for ep in range(EXPERT_PAIRS):
                first = 1 if ep == 0 else 0
                steps.begin(total)
                for u in range(SLOTS * first):
                    expert_step((0, 0, u))
                total += steps.n
                with dve.Fori(first, TURNS - 1) as i:
                    steps.begin((i - first) * FFN_LOOP_STEPS + total)
                    for u in range(SLOTS):
                        expert_step((ep, i, u))
                    assert steps.n == FFN_LOOP_STEPS, steps.n
                total += (TURNS - 1 - first) * FFN_LOOP_STEPS
                steps.begin(total)
                for u in range(SLOTS):
                    expert_step((ep, TURNS - 1, u))
                total += steps.n


def constants():
    import numpy as np

    c = np.zeros((P, CONST_COLS), np.float32)

    def put(name, value):
        c[:, CONST[name][0]:CONST[name][1]] = value

    p = np.arange(P)
    put("ident", np.eye(P))
    put("causal", p[:, None] <= p[None, :])
    pos = np.arange(NODES, dtype=np.float32)[:, None]
    div = np.exp(np.arange(0, D, 2, dtype=np.float32) * np.float32(-np.log(10000.0) / D))
    pe = np.zeros((NODES, D), np.float32)
    pe[:, 0::2], pe[:, 1::2] = np.sin(pos * div), np.cos(pos * div)
    put("position", np.concatenate([pe.T, pe.T]))
    put("nodes", np.arange(NODES)[None])
    first = np.array([first_token(k) for k in range(CHUNKS)])
    put("rnorm", 1 / np.sqrt((first[None] + p[:, None] + 1.0) * PHASES))
    put("expert_less_8", np.arange(EXPERTS)[None] - 8)
    put("slot_base", np.arange(EXPERTS)[None] * CAPACITY - 1)
    put("carry", (np.arange(EXPERTS * ROWS) % ROWS != 0)[None])
    put("token", np.repeat(first, 2)[None] + np.tile([0, L], CHUNKS)[None] + p[:, None])
    cosine = (p % D < PHASES)
    put("fold", np.where(cosine, -1, 1)[:, None])
    put("sin_scale", np.where(cosine, -PI, PI)[:, None])
    put("sin_bias", np.where(cosine, PI / 2, 0)[:, None])
    return c


def kernel(**inputs):
    import numpy as np
    import concourse.bacc as bacc
    from concourse.bass_utils import run_bass_kernel_spmd

    short = {"x": "x", "txt": "txt", "L0_tok_edge_index": "edge_index"}
    for n in ("W_embed", "b_embed", "W_gcn", "b_gcn", "W_out", "b_out"):
        short["L0_tok_" + n] = n
    for n in ("kb1", "kb2", "qb1", "qb2", "vb"):
        short["L0_attn_" + n] = n
    for n in ("gate_w", "gate_b", "w1", "b1", "w2", "b2"):
        short["L0_ffn_" + n] = n
    arrays = {v: np.ascontiguousarray(inputs[k]) for k, v in short.items()}
    for n in ("kw1", "kw2", "qw1", "qw2", "vw"):
        arrays[n + "T"] = np.ascontiguousarray(np.transpose(inputs["L0_attn_" + n]))
    arrays["constants"] = constants()

    nc = bacc.Bacc("TRN2", target_bir_lowering=False, num_devices=1)
    d = {n: nc.dram_tensor("in_" + n, a.shape, mybir.dt.from_np(a.dtype), kind="ExternalInput").ap()
         for n, a in arrays.items()}
    d["out"] = nc.dram_tensor("out_rows", (BATCH, L, D), F32, kind="ExternalOutput").ap()
    build(nc, d)
    r = run_bass_kernel_spmd(nc, [{"in_" + n: a for n, a in arrays.items()}], core_ids=[0])
    return r.results[0]["out_rows"]
```
